# Optimizing a Trainium2 kernel written in Bass

```python
import numpy as np
import jax
import jax.numpy as jnp

def _softmax(x, axis=-1):
    return jax.nn.softmax(x, axis=axis)

def _gelu(x):
    return jax.nn.gelu(x, approximate=True)

def _silu(x):
    return jax.nn.silu(x)

def _sigmoid(x):
    return jax.nn.sigmoid(x)

def _layernorm(x, axis=-1, eps=1e-05):
    m = jnp.mean(x, axis=axis, keepdims=True)
    v = jnp.var(x, axis=axis, keepdims=True)
    return (x - m) / jnp.sqrt(v + eps)

def _scatter_add(tgt, idx, src, axis=0):
    return tgt.at[idx].add(src)

def _segment_sum(src, seg, n):
    return jax.ops.segment_sum(src, seg, n)
kernel_name = 'mk_xattn_ffn_d1_seqx_r4_3e3110'

def setup_inputs(seed: int=0):
    np.random.seed(seed)
    _w = jnp.asarray

    def _rec_inputs():
        import jax
        import jax.numpy as jnp
        _rk = jax.random.key(seed)
        x = 7.22e-05 + 1 * jax.random.normal(jax.random.fold_in(_rk, 1), (1, 2048, 256), jnp.float32)
        _lenS = 2048 - jax.random.randint(jax.random.fold_in(_rk, 7), (1,), 0, max(1, 2048 // 4) + 1, jnp.int32)
        _lenS2 = 1601 - jax.random.randint(jax.random.fold_in(_rk, 8), (1,), 0, max(1, 1601 // 4) + 1, jnp.int32)
        _ctx_1024P = jax.random.normal(jax.random.fold_in(_rk, 11), (1, 16, 256), jnp.float32)
        _ctx_1024c = jax.random.dirichlet(jax.random.fold_in(_rk, 511), 0.3 * jnp.ones((16,), jnp.float32), (1, 1601))
        _ctx_1024t = jnp.einsum('bsk,bkd->bsd', _ctx_1024c, _ctx_1024P)
        _ctx_1024t = _ctx_1024t * jax.lax.rsqrt(jnp.mean(jnp.square(_ctx_1024t)) + 1e-12) * 0.953939
        ctx_1024 = 4.13588e-05 + 0.999923 * (_ctx_1024t + 0.3 * jax.random.normal(jax.random.fold_in(_rk, 611), (1, 1601, 256), jnp.float32))
        return (x, ctx_1024)
    x, ctx_1024 = _rec_inputs()

    def _L0_xattn_setup():
        import math
        import jax, jax.numpy as jnp
        import numpy as np
        H = 16
        D_MODEL = 256
        DK = D_MODEL // H
        K_FACTOR = 2

        def _time_delay_agg_inference(v, corr):
            B, _, _, L = v.shape
            top_k = min(int(K_FACTOR * math.log(L)), L)
            mean_value = jnp.mean(corr, axis=(1, 2))
            weights, delay = jax.lax.top_k(mean_value, top_k)
            tmp_corr = jax.nn.softmax(weights, axis=-1)
            idx = (delay[:, :, None] + jnp.arange(L)) % L
            gathered = jnp.take_along_axis(v[:, None], idx[:, :, None, None, :], axis=-1)
            return jnp.einsum('bk,bkhdl->bhdl', tmp_corr, gathered)
        key = jax.random.key(seed)
        ks = jax.random.split(key, 11)
        B, L, D = (4, 512, D_MODEL)
        s = 1.0 / math.sqrt(D)
        return {'queries': jax.random.normal(ks[0], (B, L, D), jnp.float32), 'keys': jax.random.normal(ks[1], (B, L, D), jnp.float32), 'values': jax.random.normal(ks[2], (B, L, D), jnp.float32), 'Wq': jax.random.normal(ks[3], (D, H * DK), jnp.float32) * s, 'bq': jnp.zeros((H * DK,), jnp.float32), 'Wk': jax.random.normal(ks[4], (D, H * DK), jnp.float32) * s, 'bk': jnp.zeros((H * DK,), jnp.float32), 'Wv': jax.random.normal(ks[5], (D, H * DK), jnp.float32) * s, 'bv': jnp.zeros((H * DK,), jnp.float32), 'Wo': jax.random.normal(ks[6], (H * DK, D), jnp.float32) * s, 'bo': jnp.zeros((D,), jnp.float32)}
    _L0_xattn_all = _L0_xattn_setup()
    _L0_xattn_in = {k: v for k, v in _L0_xattn_all.items() if k in ('Wq', 'bq', 'Wk', 'bk', 'Wv', 'bv', 'Wo', 'bo')}
    del _L0_xattn_all

    def _L0_ffn_setup():
        import jax, jax.numpy as jnp
        import numpy as np

        def _ste(w, w_q):
            return w + jax.lax.stop_gradient(w_q - w)

        def quantize_w8_per(w, axis):
            amax = jnp.clip(jnp.max(jnp.abs(w), axis=axis, keepdims=True), 1e-08, None)
            scale = 127.0 / amax
            w_q = jnp.clip(jnp.round(w * scale), -128.0, 127.0) / scale
            return _ste(w, w_q)

        def quantize_a16(x):
            amax = jnp.clip(jnp.max(jnp.abs(x)), 1e-08, None)
            scale = 32767.0 / amax
            x_q = jnp.clip(jnp.round(x * scale), -32768.0, 32767.0) / scale
            return _ste(x, x_q)
        key = jax.random.key(seed)
        k1, k2, k3 = jax.random.split(key, 3)
        d_model, d_ff = (256, 1024)
        x = jax.random.normal(k1, (4, 512, d_model), dtype=jnp.float32)
        W_in = jax.random.normal(k2, (d_model, d_ff), dtype=jnp.float32) / np.sqrt(d_model)
        b_in = jnp.zeros((d_ff,), dtype=jnp.float32)
        W_out = jax.random.normal(k3, (d_ff, d_model), dtype=jnp.float32) / np.sqrt(d_ff)
        b_out = jnp.zeros((d_model,), dtype=jnp.float32)
        return {'x': x, 'W_in': W_in, 'b_in': b_in, 'W_out': W_out, 'b_out': b_out}
    _L0_ffn_all = _L0_ffn_setup()
    _L0_ffn_in = {k: v for k, v in _L0_ffn_all.items() if k in ('W_in', 'b_in', 'W_out', 'b_out')}
    del _L0_ffn_all
    return {'x': x, 'ctx_1024': ctx_1024, 'L0_xattn_Wq': _L0_xattn_in['Wq'], 'L0_xattn_bq': _L0_xattn_in['bq'], 'L0_xattn_Wk': _L0_xattn_in['Wk'], 'L0_xattn_bk': _L0_xattn_in['bk'], 'L0_xattn_Wv': _L0_xattn_in['Wv'], 'L0_xattn_bv': _L0_xattn_in['bv'], 'L0_xattn_Wo': _L0_xattn_in['Wo'], 'L0_xattn_bo': _L0_xattn_in['bo'], 'L0_ffn_W_in': _L0_ffn_in['W_in'], 'L0_ffn_b_in': _L0_ffn_in['b_in'], 'L0_ffn_W_out': _L0_ffn_in['W_out'], 'L0_ffn_b_out': _L0_ffn_in['b_out']}

def reference(x, ctx_1024, L0_xattn_Wq, L0_xattn_bq, L0_xattn_Wk, L0_xattn_bk, L0_xattn_Wv, L0_xattn_bv, L0_xattn_Wo, L0_xattn_bo, L0_ffn_W_in, L0_ffn_b_in, L0_ffn_W_out, L0_ffn_b_out):
    import jax
    import jax.numpy as jnp

    def _L0_xattn_ref(queries, keys, values, Wq, bq, Wk, bk, Wv, bv, Wo, bo):
        import math
        import jax, jax.numpy as jnp
        import numpy as np
        H = 16
        D_MODEL = 256
        DK = D_MODEL // H
        K_FACTOR = 2

        def _time_delay_agg_inference(v, corr):
            B, _, _, L = v.shape
            top_k = min(int(K_FACTOR * math.log(L)), L)
            mean_value = jnp.mean(corr, axis=(1, 2))
            weights, delay = jax.lax.top_k(mean_value, top_k)
            tmp_corr = jax.nn.softmax(weights, axis=-1)
            idx = (delay[:, :, None] + jnp.arange(L)) % L
            gathered = jnp.take_along_axis(v[:, None], idx[:, :, None, None, :], axis=-1)
            return jnp.einsum('bk,bkhdl->bhdl', tmp_corr, gathered)
        B, Lq, _ = queries.shape
        Lk = keys.shape[1]
        q = (queries @ Wq + bq).reshape(B, Lq, H, DK)
        k = (keys @ Wk + bk).reshape(B, Lk, H, DK)
        v = (values @ Wv + bv).reshape(B, Lk, H, DK)
        if Lq > Lk:
            pad = ((0, 0), (0, Lq - Lk), (0, 0), (0, 0))
            k = jnp.pad(k, pad)
            v = jnp.pad(v, pad)
        else:
            k = k[:, :Lq]
            v = v[:, :Lq]
        qt = jnp.transpose(q, (0, 2, 3, 1))
        kt = jnp.transpose(k, (0, 2, 3, 1))
        vt = jnp.transpose(v, (0, 2, 3, 1))
        qf = jnp.fft.rfft(qt)
        kf = jnp.fft.rfft(kt)
        c = qf.real * kf.real + 1j * -(qf.imag * kf.imag)
        corr = jnp.fft.irfft(c, n=Lq).astype(qt.dtype)
        agg = _time_delay_agg_inference(vt, corr)
        out = jnp.transpose(agg, (0, 3, 1, 2)).reshape(B, Lq, H * DK)
        return out @ Wo + bo

    def _L0_ffn_ref(x, W_in, b_in, W_out, b_out):
        import jax, jax.numpy as jnp
        import numpy as np

        def _ste(w, w_q):
            return w + jax.lax.stop_gradient(w_q - w)

        def quantize_w8_per(w, axis):
            amax = jnp.clip(jnp.max(jnp.abs(w), axis=axis, keepdims=True), 1e-08, None)
            scale = 127.0 / amax
            w_q = jnp.clip(jnp.round(w * scale), -128.0, 127.0) / scale
            return _ste(w, w_q)

        def quantize_a16(x):
            amax = jnp.clip(jnp.max(jnp.abs(x)), 1e-08, None)
            scale = 32767.0 / amax
            x_q = jnp.clip(jnp.round(x * scale), -32768.0, 32767.0) / scale
            return _ste(x, x_q)
        W_in_sim = quantize_w8_per(W_in, axis=0)
        W_out_sim = quantize_w8_per(W_out, axis=1)
        x_sim = quantize_a16(x)
        hidden = jax.nn.gelu(x_sim @ W_in_sim + b_in, approximate=False)
        hidden_sim = quantize_a16(hidden)
        out = hidden_sim @ W_out_sim + b_out
        return out
    x = x + _L0_xattn_ref(_layernorm(x, axis=-1), ctx_1024, ctx_1024, L0_xattn_Wq, L0_xattn_bq, L0_xattn_Wk, L0_xattn_bk, L0_xattn_Wv, L0_xattn_bv, L0_xattn_Wo, L0_xattn_bo)
    x = x + _L0_ffn_ref(_layernorm(x, axis=-1), L0_ffn_W_in, L0_ffn_b_in, L0_ffn_W_out, L0_ffn_b_out)
    return x

_drawn_inputs = setup_inputs


def setup_inputs(seed=0):
    import zlib

    import numpy as np

    out = dict(_drawn_inputs(seed))
    spreads = {'L0_xattn_bq': (0.0, 0.1),
     'L0_xattn_bk': (0.0, 0.1),
     'L0_xattn_bv': (0.0, 0.1),
     'L0_xattn_bo': (0.0, 0.1),
     'L0_ffn_b_in': (0.0, 0.1),
     'L0_ffn_b_out': (0.0, 0.1)}
    factors = {}
    for name, (base, spread) in spreads.items():
        noise = np.random.default_rng([zlib.crc32(name.encode()), seed]).standard_normal(out[name].shape)
        drawn = base * np.exp(spread * noise) if base else spread * noise
        out[name] = jnp.asarray(drawn.astype(out[name].dtype))
    for name, factor in factors.items():
        out[name] = (out[name] * factor).astype(out[name].dtype)
    return out
```

```python
import concourse.bass as bass
from concourse import mybir
from contextlib import ExitStack
import numpy as np

T = 2048
TC = 1601
D = 256
FF = 1024
NA, NB = 128, 16
NS, NG, NJ = 64, 16, 4
NM = 32
TOPK = int(2 * np.log(T))
AF = TC // NB


def shape_tables():
    a, b = np.arange(NA), np.arange(NB)
    F = np.zeros((NA, NS, 2))
    for s in range(NS):
        F[:, s, 0] = np.cos(2 * np.pi * ((s * a) % NA) / NA)
        F[:, s, 1] = -np.sin(2 * np.pi * ((s * a) % NA) / NA)
    F[:, 0, 1] = 1.0 - 2.0 * (a % 2)
    U = np.zeros((NS, NM, NB, 2))
    V = np.zeros((NS, NM, NB, 2))
    sign = np.ones((NS, NM))
    for s in range(NS):
        for m in range(NM):
            k, part = m // 2, m % 2
            if s:
                f, w = s + NA * k, 2
            elif k == 0:
                f, w, part, src = (T // 2) * part, 1, 0, 0
            elif k < 8:
                f, w, src = NA * k, 2, 0
            else:
                f, w, src = NA // 2 + NA * (k - 8), 2, 1
            th = 2 * np.pi * ((f * b) % T) / T
            c, n = np.cos(th), -np.sin(th)
            if s:
                U[s, m, :, 0], U[s, m, :, 1] = (c, -n) if part == 0 else (n, c)
            else:
                U[s, m, :, src] = c if part == 0 else n
            V[s, m] = U[s, m] * w / T
            if part:
                sign[s, m] = 1.0 if f > T // 2 else -1.0
    P = V * (sign / D)[:, :, None, None]
    UR, UI, W = np.zeros_like(U), np.zeros_like(U), np.zeros_like(V)
    for m in range(NM):
        UR[:, m], UI[:, m] = U[:, m - m % 2], U[:, m - m % 2 + 1]
        W[:, m] = -V[:, m + 1] if m % 2 == 0 else V[:, m - 1]
    UR[0, 1], UI[0, 0:2], W[0, 0:2] = U[0, 1], 0, 0
    rows = [AF + 1 if x < TC - AF * NB else AF for x in range(NB)]
    ind = np.stack([F[0:rows[x]].sum(0) for x in range(NB)], 1)

    def by_row(x):
        return x.reshape(NG, NJ, NM, 32).transpose(1, 2, 0, 3).reshape(128, -1)

    out = {
        "F": F.reshape(NA, 128),
        "UT": U.reshape(NG, NJ, NM, 32).transpose(1, 3, 0, 2).reshape(128, -1),
        "IND": ind.reshape(NG, 128).T,
        "U": by_row(U), "P": by_row(P),
        "FR": np.concatenate([F.reshape(NA, NG, NJ, 2).transpose(2, 1, 3, 0).reshape(NS, 256), np.zeros((64, 256))], 0),
        "J": np.repeat(np.eye(NJ), NM, axis=0),
        "JT": np.concatenate([np.repeat(np.eye(NJ), NM, axis=0).T, np.zeros((124, 128))], 0),
        "UR": by_row(UR), "UI": by_row(UI), "V": by_row(V), "W": by_row(W),
        "FT": F.transpose(1, 2, 0).reshape(128, NA),
        "I": np.eye(128),
        "FS": F.reshape(NA, NG, NJ, 2).transpose(0, 3, 2, 1).reshape(NA, 128),
    }
    at, pos = {}, 0
    for k, x in out.items():
        at[k] = (pos, pos + x.shape[1])
        pos += x.shape[1]
    return np.concatenate(list(out.values()), 1).astype(np.float32), at, ind.reshape(1, -1).astype(np.float32)


def build(nc, x, ctx_in, wq, wk, wvT, wo, winT, wout, cols, rows, tab, indrow, out, at):
    f32, bf16, f16 = mybir.dt.float32, mybir.dt.bfloat16, mybir.dt.float16
    ALU, ACT, AX = mybir.AluOpType, mybir.ActivationFunctionType, mybir.AxisListType
    MAGIC = 12582912.0
    TAKEN, PAST = -3.3e38, -3.0e38
    NCONST = tab.shape[1]
    es = ExitStack()
    with es:
        SL = 4096
        arena = es.enter_context(nc.sbuf_tensor("arena", [128, 9 * SL], f32))

        def slot(n, cols=SL, skip=0):
            return arena[:, n * SL + skip:n * SL + skip + cols]

        xs = slot(0)
        cx = slot(1)
        xh = slot(2)
        xt = slot(3)
        BU = slot(4, 2048).rearrange("p (g c) -> p g c", g=NG)
        NM_ = slot(4, 2048, 2048).rearrange("p (g c) -> p g c", g=NG)
        indb = slot(4, 2048, 2048)
        ct = slot(5)
        kt = slot(6)
        qt = slot(7)
        wraw = slot(8)
        H = arena[:, 1 * SL:5 * SL].rearrange("p (f t) -> p f t", f=8)
        Hhi = arena[:, 6 * SL:8 * SL].bitcast(f16).rearrange("p (f t) -> p f t", f=8)
        Hlo5 = slot(5).bitcast(f16).rearrange("p (f t) -> p f t", f=4)
        Hlo8 = slot(8).bitcast(f16).rearrange("p (f t) -> p f t", f=4)
        yhi = slot(5, 2048).bitcast(bf16).rearrange("p (h t) -> p h t", h=2)
        ylo = slot(5, 2048, 2048).bitcast(bf16).rearrange("p (h t) -> p h t", h=2)

        def sb(name, shape, dt=f32):
            return es.enter_context(nc.sbuf_tensor(name, shape, dt))

        tabs = sb("tabs", [128, NCONST])

        def tb(name, p=128):
            return tabs[0:p, at[name][0]:at[name][1]]

        def tb3(name):
            return tb(name).rearrange("p (g c) -> p g c", g=NG)

        wk_s, wq_s, wvT_s, wo_s = (sb(n, [128, 2, D]) for n in ("wk_s", "wq_s", "wvT_s", "wo_s"))
        wvo = sb("wvo", [128, 2, D])
        bvo = sb("bvo", [128, D])
        bvb = sb("bvb", [128, 2, 128])
        winq = sb("winq", [128, 2, FF], bf16)
        woutq = sb("woutq", [128, 8, D], f16)
        colv = sb("colv", [128, 14])
        rowv = sb("rowv", [128, 2 * D])
        scr = sb("scr", [128, 4, 1024])
        winq_t = scr[:, 2, :].bitcast(bf16).rearrange("p (f d) -> p f d", f=8)
        wtmp = scr[:, 3, 0:D]
        gram = scr[:, 0, 0:512].rearrange("p (g c) -> p g c", g=NG)
        pr1 = scr[:, 0, 512:1024].rearrange("p (g c) -> p g c", g=NG)
        pr2 = scr[:, 1, 0:512].rearrange("p (g c) -> p g c", g=NG)
        in4 = scr[0:NJ, 1, 512:1024]
        rowA, rowB = slot(6, T + 8)[0:1], slot(7, T + 8)[0:1]
        ins = sb("ins", [NS, NM])
        sm = sb("sm", [128, 512])
        sq = [0]

        def small(n, p=128):
            sq[0] += n
            return sm[0:p, sq[0] - n:sq[0]]

        eps, one, negM = small(1), small(1), small(1)
        bq128 = small(2)
        st = small(96).rearrange("p (b k) -> p b k", b=NB)
        mv = small(32).rearrange("p (b k) -> p b k", b=NB)
        sd, rs, nt = small(16), small(16), small(16)
        ab, mean, sel, ex, wu, wn = (small(16) for _ in range(6))
        negmx, zr, rz = small(1), small(1), small(1)
        m8a, m8b = small(8), small(8)
        r1, r2 = small(16), small(16)
        wx, wm, wom = small(8), small(8), small(8)
        rf, wg, rwg = small(8), small(1), small(1)
        ss1, ss2 = small(8), small(8)
        ym, hm, am, yb, hb = small(4), small(16), small(1), small(1), small(1)
        ysc, hsc, sc1, sc2 = small(1), small(1), small(8), small(1)
        a1, a2, a3 = small(1, 1), small(1, 1), small(1, 1)
        ones = sb("ones", [128, 128])
        identb = sb("identb", [128, 128], bf16)

        ps = es.enter_context(nc.psum_tensor("ps", [128, 8, 512], f32))

        def sem(name):
            return es.enter_context(nc.semaphore(name))

        names = ("ld_F ld_wk ld_ind ld_wq ld_x ld_tab ld_wv ld_win ld_wout ld_col ld_row "
                 "pe dve_link act_link pool_const bu_ready xb_ready x2b_ready nz_ready "
                 "xh_ready kt_ready qt_ready wvo_ready bvo_ready bvb_ready gram_a gram_d ab_ready p2_ready in4_ready "
                 "ins_in mean_ready row_in row_ready sel_in mx_ready ex_ready zr_ready wn_ready "
                 "w1_ready w4_in vh_ready vv_ready w2_ready nm_d nm_p os_a os_d x2_ready sd_ready "
                 "var_ready y_ready yt_ready am_ready a1_ready ysc_ready wintq_ready winq_ready "
                 "wom_ready wg_ready rf_ready yu_ready yhi_ready yq_ready h_ready hm_ready ha_ready hsc_ready "
                 "hu_ready hp_ready hhi_ready hq_ready o_ready out_done ct_a ct_d xt_a xt_d bq_ready past_ready identb_ready").split()
        S = {n: sem(n) for n in names}
        ld_ctx = [sem(f"ld_ctx{i}") for i in range(5)]
        ld_xs = [sem(f"ld_x{i}") for i in range(4)]
        spec_in = [sem(f"spec_in{i}") for i in range(8)]
        out_sem = [sem(f"out{i}") for i in range(8)]

        order = []
        order += [("CD", i) for i in range(8)] + [("KP", i) for i in range(8)]
        order += [("XD", i) for i in range(8)] + [("QP", i) for i in range(8)]
        order += [("GR", i) for i in range(4)] + [("WVO", 0), ("BVO", 0), ("UU", 0)]
        order += [("VP", i) for i in range(0, 2)] + [("IN", 0)]
        order += [("VP", i) for i in range(2, 6)] + [("ME", 0)]
        order += [("VP", i) for i in range(6, 8)] + [("VF", i) for i in range(8)]
        order += [("WG1", 0), ("WG2", 0), ("WB", 0), ("WB", 1)]
        order += [("MX", 0), ("ZZ", 0), ("W1", 0), ("W2", 0)]
        order += [("OO", i) for i in range(8)] + [("IV", i) for i in range(8)]
        order += [("TY", i) for i in range(8)] + [("AM1", 0), ("AM2", 0)]
        order += [("M1", i) for i in range(32)] + [("HM1", 0), ("HM2", 0)]
        order += [("M2", i) for i in range(8)]
        nth = {u: n for n, u in enumerate(order)}

        emptied = {
            "CD": lambda i: [(S["ct_a" if i % 2 == 0 else "ct_d"], i // 2 + 1)],
            "KP": lambda i: [(S["kt_ready"], i + 1)],
            "XD": lambda i: [(S["xt_a" if i % 2 == 0 else "xt_d"], i // 2 + 1)],
            "QP": lambda i: [(S["qt_ready"], i + 1)],
            "GR": lambda i: [(S["gram_a"], i + 1), (S["gram_d"], i + 1)],
            "WVO": lambda i: [(S["wvo_ready"], 1)],
            "BVO": lambda i: [(S["bvo_ready"], 1)],
            "UU": lambda i: [(S["ab_ready"], 1)],
            "VP": lambda i: [(S["vh_ready"], i + 1)],
            "IN": lambda i: [(S["in4_ready"], 1)],
            "ME": lambda i: [(S["mean_ready"], 1)],
            "VF": lambda i: [(S["vv_ready"], i + 1)],
            "WG1": lambda i: [(S["wg_ready"], 1)],
            "WG2": lambda i: [(S["rf_ready"], 1)],
            "WB": lambda i: [(S["winq_ready"], i + 1)],
            "MX": lambda i: [(S["ex_ready"], 1)],
            "ZZ": lambda i: [(S["wn_ready"], 1)],
            "W1": lambda i: [(S["w1_ready"], 1)],
            "W2": lambda i: [(S["w2_ready"], 1)],
            "OO": lambda i: [(S["os_a" if i % 2 == 0 else "os_d"], i // 2 + 1)],
            "IV": lambda i: [(S["x2_ready"], i + 1)],
            "TY": lambda i: [(S["yt_ready"], i + 1)],
            "AM1": lambda i: [(S["a1_ready"], 1)],
            "AM2": lambda i: [(S["ysc_ready"], 1)],
            "M1": lambda i: [(S["h_ready"], i + 1)],
            "HM1": lambda i: [(S["ha_ready"], 1)],
            "HM2": lambda i: [(S["hsc_ready"], 1)],
        }

        def bank(stage, i):
            return ps[:, nth[stage, i] % 8, :]

        def filled(eng, stage, i):
            eng.wait_ge(S["pe"], nth[stage, i] + 1)

        def take_bank(pe, stage, i):
            n = nth[stage, i]
            if n >= 8:
                prev, k = order[n - 8]
                for s, v in emptied[prev](k):
                    pe.wait_ge(s, v)
            return ps[:, n % 8, :]

        block = es.enter_context(nc.Block())

        @block.sync
        def _(sp):
            c3 = ctx_in[0, 0:AF * NB, :].rearrange("(a b) d -> a b d", b=NB)
            cs = cx.rearrange("p (b d) -> p b d", b=NB)
            sp.dma_start(tb("F"), tab[:, at["F"][0]:at["F"][1]]).then_inc(S["ld_F"], 16)
            sp.dma_start(cs[AF:AF + 1, 0, :], ctx_in[0, AF * NB:TC, :]).then_inc(ld_ctx[4], 16)
            for i in range(4):
                sp.dma_start(cs[0:AF, 4 * i:4 * i + 4, :], c3[:, 4 * i:4 * i + 4, :]).then_inc(ld_ctx[i], 16)
            sp.dma_start(wk_s[:], wk.rearrange("(h p) n -> p h n", p=128)).then_inc(S["ld_wk"], 16)
            sp.dma_start(colv[:], cols).then_inc(S["ld_col"], 16)
            x3 = x[0].rearrange("(a b) d -> a (b d)", b=NB)
            for i in range(4):
                sp.dma_start(xs[:, 1024 * i:1024 * i + 1024], x3[:, 1024 * i:1024 * i + 1024]).then_inc(ld_xs[i], 16)
            sp.dma_start(indb, indrow[0:1, :].to_broadcast([128, 2048])).then_inc(S["ld_ind"], 16)
            sp.dma_start(wq_s[:], wq.rearrange("(h p) n -> p h n", p=128)).then_inc(S["ld_wq"], 16)
            sp.dma_start(wvT_s[:], wvT.rearrange("(h p) n -> p h n", p=128)).then_inc(S["ld_wv"], 16)
            sp.dma_start(wo_s[:], wo.rearrange("(h p) n -> p h n", p=128)).then_inc(S["ld_wv"], 16)
            sp.dma_start(tabs[:, at["UT"][0]:NCONST], tab[:, at["UT"][0]:NCONST]).then_inc(S["ld_tab"], 16)
            sp.dma_start(rowv[:], rows[0:1, :].to_broadcast([128, 2 * D])).then_inc(S["ld_row"], 16)
            sp.dma_start(wraw[:, 0:2048].rearrange("p (f d) -> p f d", f=8),
                         winT.rearrange("(f p) d -> p f d", p=128)).then_inc(S["ld_win"], 16)
            sp.dma_start(wraw[:, 2048:4096].rearrange("p (f d) -> p f d", f=8),
                         wout.rearrange("(f p) d -> p f d", p=128)).then_inc(S["ld_wout"], 16)
            sp.wait_ge(S["in4_ready"], 1)
            sp.dma_start(ins[:], in4.rearrange("j (g c) -> j g c", g=NG)).then_inc(S["ins_in"], 16)
            sp.wait_ge(S["mean_ready"], 1)
            sp.dma_start(rowA[:, 0:T].rearrange("o (a b) -> o a b", b=NB), mean).then_inc(S["row_in"], 16)
            sp.wait_ge(S["row_ready"], 1)
            sp.dma_start(sel, rowA[:, 0:T].rearrange("o (a b) -> o a b", b=NB)).then_inc(S["sel_in"], 16)
            sp.wait_ge(S["w1_ready"], 1)
            sp.dma_start(in4.rearrange("j (g c) -> j g c", g=NG), ins[:]).then_inc(S["w4_in"], 16)
            os3 = cx.rearrange("p (g c) -> p g c", g=NG)
            or3 = ct.rearrange("p (b c) -> p b c", b=NB)
            for i in range(8):
                sp.wait_ge(S["os_a" if i % 2 == 0 else "os_d"], i // 2 + 1)
                for g in (2 * i, 2 * i + 1):
                    sp.dma_start(or3[8 * g:8 * g + 8], os3[:, g, :]).then_inc(spec_in[i], 16)
            o3 = out[0].rearrange("(a b) d -> a (b d)", b=NB)
            for i in range(8):
                sp.wait_ge(S["o_ready"], i + 1)
                sp.dma_start(o3[:, 512 * i:512 * i + 512], xs[:, 512 * i:512 * i + 512]).then_inc(S["out_done"], 16)
            sp.wait_ge(S["out_done"], 8 * 16)

        @block.gpsimd
        def _(pool):
            g = nc.gpsimd
            g.memset(ones[:], 1.0)
            g.memset(one, 1.0)
            g.memset(negM, -MAGIC)
            g.memset(eps, 1e-5)
            g.memset(BU, 0.0).then_inc(S["pool_const"], 1)
            pool.wait_ge(S["pool_const"], 1)
            pool.wait_ge(S["ld_tab"], 16)
            g.tensor_copy(identb[:], tb("I")).then_inc(S["identb_ready"], 1)
            pool.wait_ge(S["identb_ready"], 1)
            for j in range(NJ):
                q = slice(32 * j, 32 * j + 32)
                g.tensor_copy(BU[q, :, q], tb3("UT")[q]).then_inc(S["bu_ready"], 1)
                pool.wait_ge(S["bu_ready"], j + 1)
            pool.wait_ge(S["xh_ready"], 4)
            pool.wait_ge(S["ld_row"], 16)
            x3 = xs.rearrange("p (b d) -> p b d", b=NB)
            g.tensor_tensor(x3, x3, rowv[:, 0:D].unsqueeze(1).to_broadcast([128, NB, D]), ALU.add).then_inc(S["xb_ready"], 1)
            pool.wait_ge(S["xb_ready"], 1)
            pool.wait_ge(S["kt_ready"], 8)
            g.memset(NM_, 0.0).then_inc(S["nz_ready"], 1)
            pool.wait_ge(S["nz_ready"], 1)
            pool.wait_ge(S["gram_a"], 4)
            g.memset(rowA[:, T:T + 8], PAST).then_inc(S["past_ready"], 1)
            pool.wait_ge(S["past_ready"], 1)
            pool.wait_ge(S["y_ready"], 4)
            g.tensor_tensor(x3, x3, rowv[:, D:2 * D].unsqueeze(1).to_broadcast([128, NB, D]), ALU.add).then_inc(S["x2b_ready"], 1)

        def spread(buf, h, bq):
            v = buf[:, h * 2048:(h + 1) * 2048].rearrange("p (s b r) -> p b s r", b=NB, r=2)
            return v[:, 4 * bq:4 * bq + 4]

        @block.scalar
        def _(act):
            a = nc.scalar
            linked = [0]

            def link(ins_):
                linked[0] += 1
                ins_.then_inc(S["act_link"], 1)
                act.wait_ge(S["act_link"], linked[0])

            act.wait_ge(S["pool_const"], 1)
            for i in range(0, 8, 2):
                filled(act, "CD", i)
                a.copy(spread(ct, 0, i // 2), bank("CD", i).rearrange("p (b s r) -> p b s r", b=4, r=2)).then_inc(S["ct_a"], 1)
            act.wait_ge(S["var_ready"], 1)
            a.activation(sd, mv[:, :, 1], ACT.Sqrt, bias=eps).then_inc(S["sd_ready"], 1)
            act.wait_ge(S["ld_col"], 16)
            a.mul(bq128, colv[:, 2:4], float(NA)).then_inc(S["bq_ready"], 1)
            for i in range(0, 8, 2):
                filled(act, "XD", i)
                a.copy(spread(xt, 0, i // 2), bank("XD", i).rearrange("p (b s r) -> p b s r", b=4, r=2)).then_inc(S["xt_a"], 1)
            act.wait_ge(S["bq_ready"], 1)
            for i in range(8):
                h, c = i // 4, i % 4
                filled(act, "QP", i)
                dst = qt[:, h * 2048 + c * 512:h * 2048 + c * 512 + 512]
                src = bank("QP", i)
                if c == 0:
                    a.activation(dst[:, 0:32:2], src[:, 0:32:2], ACT.Identity, bias=bq128[:, h:h + 1])
                    a.copy(dst[:, 1:32:2], src[:, 1:32:2])
                    a.copy(dst[:, 32:512], src[:, 32:512]).then_inc(S["qt_ready"], 1)
                else:
                    a.copy(dst, src).then_inc(S["qt_ready"], 1)
            for i in range(4):
                filled(act, "GR", i)
                for j in (0, 1):
                    q = slice(32 * j, 32 * j + 32)
                    ins_ = a.copy(gram[q, 4 * i:4 * i + 4, :],
                                  bank("GR", i).rearrange("p (g c) -> p g c", g=4)[q, :, q])
                ins_.then_inc(S["gram_a"], 1)
            filled(act, "WVO", 0)
            a.copy(wvo[:].rearrange("p h n -> p (h n)"), bank("WVO", 0)).then_inc(S["wvo_ready"], 1)
            filled(act, "BVO", 0)
            a.copy(bvo[:], bank("BVO", 0)[:, 0:D]).then_inc(S["bvo_ready"], 1)
            filled(act, "IN", 0)
            a.copy(in4, bank("IN", 0)[0:NJ, :]).then_inc(S["in4_ready"], 1)
            for i in range(8):
                filled(act, "VF", i)
                a.copy(xt[:, 512 * i:512 * i + 512], bank("VF", i)).then_inc(S["vv_ready"], 1)
            for i in range(2):
                filled(act, "WB", i)
                a.copy(winq[:, i, :], bank("WB", i).bitcast(bf16)).then_inc(S["winq_ready"], 1)
            filled(act, "MX", 0)
            link(a.mul(negmx, bank("MX", 0)[:, 0:1], -1.0))
            a.activation(ex, mean, ACT.Exp, bias=negmx).then_inc(S["ex_ready"], 1)
            filled(act, "W1", 0)
            act.wait_ge(S["ins_in"], 16)
            a.copy(ins[:].rearrange("s (b r) -> s r b", r=2), bank("W1", 0)[0:NS, 0:32].rearrange("s (r b) -> s r b", r=2))\
             .then_inc(S["w1_ready"], 1)
            for i in range(0, 8, 2):
                filled(act, "OO", i)
                a.copy(cx[:, 512 * i:512 * i + 512], bank("OO", i)).then_inc(S["os_a"], 1)
            act.wait_ge(S["var_ready"], 2)
            a.activation(sd[:, 0:8], mv[:, 0:8, 1], ACT.Sqrt, bias=eps).then_inc(S["sd_ready"], 1)
            act.wait_ge(S["var_ready"], 3)
            a.activation(sd[:, 8:16], mv[:, 8:16, 1], ACT.Sqrt, bias=eps).then_inc(S["sd_ready"], 1)
            for i in range(8):
                filled(act, "TY", i)
                a.copy(qt.rearrange("p (h t) -> p h t", h=2)[:, :, 256 * i:256 * i + 256],
                       bank("TY", i).rearrange("p (h t) -> p h t", h=2)).then_inc(S["yt_ready"], 1)
            for c in range(4):
                act.wait_ge(S["yu_ready"], c + 1)
                a.activation(yhi[:, :, 512 * c:512 * c + 512],
                             scr[:, c, :].rearrange("p (h t) -> p h t", h=2), ACT.Identity, bias=negM)\
                 .then_inc(S["yhi_ready"], 1)
            act.wait_ge(S["ysc_ready"], 1)
            for n in range(32):
                c, f = n // 8, n % 8
                filled(act, "M1", n)
                a.activation(H[:, f, 512 * c:512 * c + 512], bank("M1", n), ACT.Gelu,
                             bias=colv[:, 6 + f:7 + f], scale=sc1[:, f:f + 1]).then_inc(S["h_ready"], 1)
            for n in range(16):
                c, f = n // 4, 2 * (n % 4)
                act.wait_ge(S["hp_ready"], n + 1)
                a.copy(Hhi[:, f:f + 2, 512 * c:512 * c + 512],
                       scr[:, n % 4, :].rearrange("p (f t) -> p f t", f=2)).then_inc(S["hhi_ready"], 1)

        @block.vector
        def _(dve):
            v = nc.vector
            linked = [0]

            def link(ins_):
                linked[0] += 1
                ins_.then_inc(S["dve_link"], 1)
                dve.wait_ge(S["dve_link"], linked[0])

            x3 = xs.rearrange("p (b d) -> p b d", b=NB)
            xh3 = xh.rearrange("p (b d) -> p b d", b=NB)
            for i in range(4):
                dve.wait_ge(ld_xs[i], 16)
                if i == 0:
                    for k in range(1, 8, 2):
                        filled(dve, "CD", k)
                        v.tensor_copy(spread(ct, 1, k // 2), bank("CD", k).rearrange("p (b s r) -> p b s r", b=4, r=2))\
                         .then_inc(S["ct_d"], 1)
                for b in range(4 * i, 4 * i + 4):
                    ins_ = v.bn_stats(st[:, b, :], x3[:, b, :])
            link(ins_)
            for b in range(NB):
                ins_ = v.bn_aggr(mv[:, b, :], st[:, b, :])
            ins_.then_inc(S["var_ready"], 1)
            dve.wait_ge(S["sd_ready"], 1)
            link(v.reciprocal(rs, sd))

            def newton(lo, hi):
                r, n_, w = rs[:, lo:hi], nt[:, lo:hi], mv[:, lo:hi, 1]
                link(v.tensor_tensor(n_, r, r, ALU.mult))
                link(v.scalar_tensor_tensor(out=n_, in0=w, scalar=1e-5, in1=n_, op0=ALU.add, op1=ALU.mult))
                link(v.tensor_scalar(n_, n_, -0.5, 1.5, ALU.mult, ALU.add))
                link(v.tensor_tensor(r, r, n_, ALU.mult))

            newton(0, NB)
            for b in range(NB):
                ins_ = v.tensor_scalar(xh3[:, b, :], x3[:, b, :], mv[:, b, 0:1], rs[:, b:b + 1], ALU.subtract, ALU.mult)
                if b % 4 == 3:
                    ins_.then_inc(S["xh_ready"], 1)
            dve.wait_ge(S["ld_ind"], 16)
            dve.wait_ge(S["ld_col"], 16)
            v.tensor_copy(bvb[:], colv[:, 4:6].unsqueeze(2).to_broadcast([128, 2, 128])).then_inc(S["bvb_ready"], 1)
            for i in range(8):
                h, c = i // 4, i % 4
                filled(dve, "KP", i)
                v.scalar_tensor_tensor(out=kt[:, h * 2048 + c * 512:h * 2048 + c * 512 + 512],
                                       in0=indb[:, c * 512:c * 512 + 512], scalar=colv[:, h:h + 1],
                                       in1=bank("KP", i), op0=ALU.mult, op1=ALU.add).then_inc(S["kt_ready"], 1)
            for k in range(1, 8, 2):
                filled(dve, "XD", k)
                v.tensor_copy(spread(xt, 1, k // 2), bank("XD", k).rearrange("p (b s r) -> p b s r", b=4, r=2))\
                 .then_inc(S["xt_d"], 1)
            dve.wait_ge(S["ld_win"], 16)
            win3 = wraw[:, 0:2048].rearrange("p (f d) -> p f d", f=8)
            wou3 = wraw[:, 2048:4096].rearrange("p (f d) -> p f d", f=8)
            link(v.tensor_reduce(wx, win3, AX.X, ALU.max, apply_absolute_value=True))
            link(v.tensor_scalar(wx, wx, 1e-8, None, ALU.max))
            link(v.reciprocal(ss1, wx))
            link(v.tensor_scalar(ss1, ss1, 127.0, None, ALU.mult))
            for f in range(8):
                link(v.tensor_scalar(wtmp, win3[:, f, :], ss1[:, f:f + 1], MAGIC, ALU.mult, ALU.add))
                link(v.tensor_scalar(winq_t[:, f, :], wtmp, MAGIC, None, ALU.subtract))
            dve.wait_ge(S["ld_wout"], 16)
            link(v.tensor_reduce(wom, wou3, AX.X, ALU.max, apply_absolute_value=True))
            link(v.tensor_scalar(wom, wom, 1e-8, None, ALU.max))
            link(v.reciprocal(ss2, wom))
            link(v.tensor_scalar(ss2, ss2, 127.0, None, ALU.mult))
            for f in range(8):
                link(v.tensor_scalar(wtmp, wou3[:, f, :], ss2[:, f:f + 1], MAGIC, ALU.mult, ALU.add))
                link(v.tensor_scalar(woutq[:, f, :], wtmp, MAGIC, None, ALU.subtract))
            v.tensor_reduce(wg, wom, AX.X, ALU.max).then_inc(S["wom_ready"], 1)

            for i in range(4):
                filled(dve, "GR", i)
                for j in (2, 3):
                    q = slice(32 * j, 32 * j + 32)
                    ins_ = v.tensor_copy(gram[q, 4 * i:4 * i + 4, :],
                                         bank("GR", i).rearrange("p (g c) -> p g c", g=4)[q, :, q])
                ins_.then_inc(S["gram_d"], 1)
            filled(dve, "UU", 0)
            link(v.tensor_tensor(pr1, bank("UU", 0).rearrange("p (g c) -> p g c", g=NG), tb3("U"), ALU.mult))
            link(v.tensor_reduce(ab, pr1, AX.X, ALU.add))
            v.tensor_tensor(pr2, tb3("P"), ab.unsqueeze(2).to_broadcast([128, NG, 32]), ALU.mult)\
             .then_inc(S["ab_ready"], 1)

            def vproj(i):
                filled(dve, "VP", i)
                for k in range(2):
                    gg = 2 * i + k
                    ins_ = v.scalar_tensor_tensor(out=xh[:, 256 * gg:256 * gg + 256], in0=bvo[:],
                                                  scalar=tb("IND")[:, gg:gg + 1],
                                                  in1=bank("VP", i)[:, 256 * k:256 * k + 256],
                                                  op0=ALU.mult, op1=ALU.add)
                ins_.then_inc(S["vh_ready"], 1)

            dve.wait_ge(S["bvo_ready"], 1)
            for i in range(6):
                vproj(i)
            filled(dve, "ME", 0)
            v.tensor_copy(mean, bank("ME", 0)[:, 0:NB]).then_inc(S["mean_ready"], 1)
            for i in range(6, 8):
                vproj(i)
            dve.wait_ge(S["row_in"], 16)
            link(v.max(m8a[0:1, :], rowA[:, 0:T]))
            dve.wait_ge(S["past_ready"], 1)
            link(v.match_replace(rowB[:, :], m8a[0:1, :], rowA[:, :], TAKEN))
            link(v.max(m8b[0:1, :], rowB[:, 0:T]))
            link(v.memset(m8b[0:1, TOPK - 8:8], PAST))
            v.match_replace(rowA[:, :], m8b[0:1, :], rowB[:, :], TAKEN).then_inc(S["row_ready"], 1)
            filled(dve, "WG1", 0)
            v.reduce_max(a1, bank("WG1", 0)[0:1, 0:128], AX.X).then_inc(S["wg_ready"], 1)
            filled(dve, "WG2", 0)
            link(v.tensor_copy(wg, bank("WG2", 0)[:, 0:1]))
            link(v.reciprocal(rwg, wg))
            v.tensor_scalar(rf, wom, rwg, None, ALU.mult).then_inc(S["rf_ready"], 1)
            dve.wait_ge(S["sel_in"], 16)
            dve.wait_ge(S["ex_ready"], 1)
            link(v.tensor_scalar(sel, sel, 0.5 * (TAKEN + PAST), None, ALU.is_le))
            link(v.tensor_tensor(wu, sel, ex, ALU.mult))
            v.reduce_sum(zr, wu, AX.X).then_inc(S["zr_ready"], 1)
            filled(dve, "ZZ", 0)
            link(v.reciprocal(rz, bank("ZZ", 0)[:, 0:1]))
            v.tensor_scalar(wn, wu, rz, None, ALU.mult).then_inc(S["wn_ready"], 1)
            filled(dve, "W2", 0)
            w2 = bank("W2", 0).rearrange("p (g c) -> p g c", g=NG)
            v.tensor_tensor(pr1, w2, tb3("UR"), ALU.mult)
            link(v.tensor_tensor(pr2, w2, tb3("UI"), ALU.mult))
            v.tensor_reduce(r1, pr1, AX.X, ALU.add)
            link(v.tensor_reduce(r2, pr2, AX.X, ALU.add))
            v.tensor_tensor(pr1, tb3("V"), r1.unsqueeze(2).to_broadcast([128, NG, 32]), ALU.mult)
            link(v.tensor_tensor(pr2, tb3("W"), r2.unsqueeze(2).to_broadcast([128, NG, 32]), ALU.mult))
            dve.wait_ge(S["nz_ready"], 1)
            for j in range(NJ):
                q = slice(32 * j, 32 * j + 32)
                dst = NM_[q, :, q].rearrange("p g (r b) -> p g b r", r=2)
                ins_ = v.tensor_tensor(dst, pr1[q].rearrange("p g (b r) -> p g b r", r=2),
                                       pr2[q].rearrange("p g (b r) -> p g b r", r=2), ALU.add)
            ins_.then_inc(S["w2_ready"], 1)
            for i in range(1, 8, 2):
                filled(dve, "OO", i)
                v.tensor_copy(cx[:, 512 * i:512 * i + 512], bank("OO", i)).then_inc(S["os_d"], 1)
            y3 = kt.rearrange("p (b d) -> p b d", b=NB)
            dve.wait_ge(S["xb_ready"], 1)
            for half in range(2):
                for i in range(4 * half, 4 * half + 4):
                    filled(dve, "IV", i)
                    v.tensor_tensor(xs[:, 512 * i:512 * i + 512], bank("IV", i), xs[:, 512 * i:512 * i + 512], ALU.add)\
                     .then_inc(S["x2_ready"], 1)
                    dve.wait_ge(S["x2_ready"], i + 1)
                    for b in (2 * i, 2 * i + 1):
                        ins_ = v.bn_stats(st[:, b, :], x3[:, b, :])
                link(ins_)
                for b in range(8 * half, 8 * half + 8):
                    ins_ = v.bn_aggr(mv[:, b, :], st[:, b, :])
                ins_.then_inc(S["var_ready"], 1)
            for half in range(2):
                dve.wait_ge(S["sd_ready"], 2 + half)
                link(v.reciprocal(rs[:, 8 * half:8 * half + 8], sd[:, 8 * half:8 * half + 8]))
                newton(8 * half, 8 * half + 8)
                for b in range(8 * half, 8 * half + 8):
                    ins_ = v.tensor_scalar(y3[:, b, :], x3[:, b, :], mv[:, b, 0:1], rs[:, b:b + 1], ALU.subtract, ALU.mult)
                    if b % 4 == 3:
                        k = b // 4
                        ins_.then_inc(S["y_ready"], 1)
                        dve.wait_ge(S["y_ready"], k + 1)
                        ins_ = v.tensor_reduce(ym[:, k:k + 1], y3[:, 4 * k:4 * k + 4, :].rearrange("p b d -> p (b d)"), AX.X, ALU.max,
                                               apply_absolute_value=True)
            link(ins_)
            v.reduce_max(am, ym, AX.X).then_inc(S["am_ready"], 1)
            filled(dve, "AM1", 0)
            link(v.reduce_max(a2, bank("AM1", 0)[0:1, 0:128], AX.X))
            v.tensor_scalar(a2, a2, 1e-8, None, ALU.max).then_inc(S["a1_ready"], 1)
            filled(dve, "AM2", 0)
            link(v.tensor_copy(yb, bank("AM2", 0)[:, 0:1]))
            link(v.reciprocal(ysc, yb))
            link(v.tensor_scalar(ysc, ysc, 32767.0, None, ALU.mult))
            link(v.tensor_scalar(yb, yb, 1.0 / 32767.0, 1.0 / 127.0, ALU.mult, ALU.mult))
            v.tensor_scalar(sc1, wx, yb, None, ALU.mult).then_inc(S["ysc_ready"], 1)
            dve.wait_ge(S["yt_ready"], 8)
            yt3 = qt.rearrange("p (h t) -> p h t", h=2)

            def y_round(c):
                v.tensor_scalar(scr[:, c, :].rearrange("p (h t) -> p h t", h=2), yt3[:, :, 512 * c:512 * c + 512],
                                ysc, MAGIC, ALU.mult, ALU.add).then_inc(S["yu_ready"], 1)

            y_round(0)
            for c in range(4):
                if c < 3:
                    y_round(c + 1)
                dve.wait_ge(S["yhi_ready"], c + 1)
                v.scalar_tensor_tensor(out=ylo[:, :, 512 * c:512 * c + 512],
                                       in0=scr[:, c, :].rearrange("p (h t) -> p h t", h=2), scalar=MAGIC,
                                       in1=yhi[:, :, 512 * c:512 * c + 512],
                                       op0=ALU.subtract, op1=ALU.subtract).then_inc(S["yq_ready"], 1)
            for n in range(16):
                c, f = n // 4, 2 * (n % 4)
                dve.wait_ge(S["h_ready"], 2 * n + 2)
                ins_ = v.tensor_reduce(hm[:, n:n + 1], H[:, f:f + 2, 512 * c:512 * c + 512], AX.XY, ALU.max,
                                       apply_absolute_value=True)
            link(ins_)
            v.reduce_max(am, hm, AX.X).then_inc(S["hm_ready"], 1)
            filled(dve, "HM1", 0)
            link(v.reduce_max(a3, bank("HM1", 0)[0:1, 0:128], AX.X))
            v.tensor_scalar(a3, a3, 1e-8, None, ALU.max).then_inc(S["ha_ready"], 1)
            filled(dve, "HM2", 0)
            link(v.tensor_copy(hb, bank("HM2", 0)[:, 0:1]))
            link(v.reciprocal(hsc, hb))
            link(v.tensor_scalar(hsc, hsc, 32767.0, None, ALU.mult))
            link(v.tensor_scalar(sc2, hb, 1.0 / 32767.0, 1.0 / 127.0, ALU.mult, ALU.mult))
            v.tensor_scalar(sc2, sc2, wg, None, ALU.mult).then_inc(S["hsc_ready"], 1)

            def lo_of(n):
                c, f = n // 4, 2 * (n % 4)
                dve.wait_ge(S["hhi_ready"], n + 1)
                part = (Hlo5 if f < 4 else Hlo8)[:, f % 4:f % 4 + 2, 512 * c:512 * c + 512]
                v.tensor_tensor(part, scr[:, n % 4, :].rearrange("p (f t) -> p f t", f=2),
                                Hhi[:, f:f + 2, 512 * c:512 * c + 512], ALU.subtract).then_inc(S["hq_ready"], 1)

            def final(i):
                filled(dve, "M2", i)
                v.scalar_tensor_tensor(out=xs[:, 512 * i:512 * i + 512], in0=bank("M2", i), scalar=sc2,
                                       in1=xs[:, 512 * i:512 * i + 512], op0=ALU.mult, op1=ALU.add)\
                 .then_inc(S["o_ready"], 1)

            dve.wait_ge(S["x2b_ready"], 1)
            for n in range(16):
                c, f = n // 4, 2 * (n % 4)
                if n >= 4:
                    dve.wait_ge(S["hq_ready"], n - 3)
                u = scr[:, n % 4, :]
                link(v.tensor_scalar(u.rearrange("p (f t) -> p f t", f=2), H[:, f:f + 2, 512 * c:512 * c + 512],
                                     hsc, MAGIC, ALU.mult, ALU.add))
                v.tensor_scalar(u[:, 0:512], u[:, 0:512], MAGIC, rf[:, f:f + 1], ALU.subtract, ALU.mult)
                v.tensor_scalar(u[:, 512:1024], u[:, 512:1024], MAGIC, rf[:, f + 1:f + 2], ALU.subtract, ALU.mult)\
                 .then_inc(S["hp_ready"], 1)
                if n >= 1:
                    lo_of(n - 1)
                if n % 4 == 3 and n > 4:
                    final(2 * (n // 4) - 2)
                    final(2 * (n // 4) - 1)
            lo_of(15)
            final(6)
            final(7)

        @block.tensor
        def _(pe):
            t = nc.tensor
            F = tb("F")

            def done(ins_):
                ins_.then_inc(S["pe"], 1)

            pe.wait_ge(S["ld_F"], 16)
            pe.wait_ge(ld_ctx[4], 16)
            for i in range(8):
                bq, h = i // 2, i % 2
                if h == 0:
                    pe.wait_ge(ld_ctx[bq], 16)
                o = take_bank(pe, "CD", i)
                for k in range(4):
                    b = 4 * bq + k
                    n = AF + 1 if b < TC - AF * NB else AF
                    last = t.matmul(o[:, 128 * k:128 * k + 128], cx[0:n, 256 * b + 128 * h:256 * b + 128 * h + 128],
                                    F[0:n, :], start=True, stop=True)
                done(last)
            pe.wait_ge(S["ld_wk"], 16)
            pe.wait_ge(S["ct_a"], 4)
            pe.wait_ge(S["ct_d"], 4)
            for i in range(8):
                h, c = i // 4, i % 4
                o = take_bank(pe, "KP", i)
                for k in range(2):
                    last = t.matmul(o, wk_s[:, k, 128 * h:128 * h + 128], ct[:, 2048 * k + 512 * c:2048 * k + 512 * c + 512],
                                    start=(k == 0), stop=(k == 1))
                done(last)
            for i in range(8):
                bq, h = i // 2, i % 2
                if h == 0:
                    pe.wait_ge(S["xh_ready"], bq + 1)
                o = take_bank(pe, "XD", i)
                for k in range(4):
                    b = 4 * bq + k
                    last = t.matmul(o[:, 128 * k:128 * k + 128], xh[:, 256 * b + 128 * h:256 * b + 128 * h + 128],
                                    F, start=True, stop=True)
                done(last)
            pe.wait_ge(S["ld_wq"], 16)
            pe.wait_ge(S["xt_a"], 4)
            pe.wait_ge(S["xt_d"], 4)
            for i in range(8):
                h, c = i // 4, i % 4
                o = take_bank(pe, "QP", i)
                for k in range(2):
                    last = t.matmul(o, wq_s[:, k, 128 * h:128 * h + 128], xt[:, 2048 * k + 512 * c:2048 * k + 512 * c + 512],
                                    start=(k == 0), stop=(k == 1))
                done(last)
            pe.wait_ge(S["kt_ready"], 8)
            pe.wait_ge(S["qt_ready"], 8)
            for i in range(4):
                o = take_bank(pe, "GR", i)
                for m in range(4):
                    g = 4 * i + m
                    for k in range(2):
                        c0 = 2048 * k + 128 * g
                        last = t.matmul(o[:, 128 * m:128 * m + 128], kt[:, c0:c0 + 128], qt[:, c0:c0 + 128],
                                        start=(k == 0), stop=(k == 1))
                done(last)
            pe.wait_ge(S["ld_wv"], 32)
            o = take_bank(pe, "WVO", 0)
            for h in range(2):
                for k in range(2):
                    last = t.matmul(o[:, 256 * h:256 * h + 256], wvT_s[:, k, 128 * h:128 * h + 128], wo_s[:, k, :],
                                    start=(k == 0), stop=(k == 1))
            done(last)
            pe.wait_ge(S["bvb_ready"], 1)
            o = take_bank(pe, "BVO", 0)
            for k in range(2):
                last = t.matmul(o[:, 0:D], bvb[:, k, :], wo_s[:, k, :], start=(k == 0), stop=(k == 1))
            done(last)
            pe.wait_ge(S["bu_ready"], NJ)
            pe.wait_ge(S["gram_a"], 4)
            pe.wait_ge(S["gram_d"], 4)
            o = take_bank(pe, "UU", 0)
            for g in range(NG):
                last = t.matmul(o[:, 32 * g:32 * g + 32], BU[:, g, :], gram[:, g, :], start=True, stop=True)
            done(last)

            def vproj(i):
                o = take_bank(pe, "VP", i)
                for m in range(2):
                    for k in range(2):
                        c0 = 2048 * k + 128 * (2 * i + m)
                        last = t.matmul(o[:, 256 * m:256 * m + 256], ct[:, c0:c0 + 128], wvo[:, k, :],
                                        start=(k == 0), stop=(k == 1))
                done(last)

            pe.wait_ge(S["wvo_ready"], 1)
            vproj(0)
            vproj(1)
            pe.wait_ge(S["ab_ready"], 1)
            o = take_bank(pe, "IN", 0)
            done(t.matmul(o[0:NJ, :], tb("J"), pr2.rearrange("p g c -> p (g c)"), start=True, stop=True))
            for i in range(2, 6):
                vproj(i)
            pe.wait_ge(S["ins_in"], 16)
            o = take_bank(pe, "ME", 0)
            for r in range(2):
                last = t.matmul(o[:, 0:NB], tb("FR", NS)[:, 128 * r:128 * r + 128], ins[:, r:NM:2],
                                start=(r == 0), stop=(r == 1))
            done(last)
            for i in range(6, 8):
                vproj(i)
            for i in range(8):
                pe.wait_ge(S["vh_ready"], i + 1)
                o = take_bank(pe, "VF", i)
                for m in range(2):
                    g = 2 * i + m
                    last = t.matmul(o[:, 256 * m:256 * m + 256], BU[:, g, :], xh[:, 256 * g:256 * g + 256],
                                    start=True, stop=True)
                done(last)
            pe.wait_ge(S["wom_ready"], 1)
            o = take_bank(pe, "WG1", 0)
            done(t.transpose(o[0:1, 0:128], wg, tb("I")))
            pe.wait_ge(S["wg_ready"], 1)
            o = take_bank(pe, "WG2", 0)
            done(t.matmul(o[:, 0:1], ones[0:1, :], a1, start=True, stop=True))
            for h in range(2):
                o = take_bank(pe, "WB", h).bitcast(bf16)
                for f in range(8):
                    last = t.transpose(o[:, 128 * f:128 * f + 128], winq_t[:, f, 128 * h:128 * h + 128], identb[:])
                done(last)
            pe.wait_ge(S["row_ready"], 1)
            o = take_bank(pe, "MX", 0)
            done(t.matmul(o[:, 0:1], ones[0:1, :], m8a[0:1, 0:1], start=True, stop=True))
            pe.wait_ge(S["zr_ready"], 1)
            o = take_bank(pe, "ZZ", 0)
            done(t.matmul(o[:, 0:1], ones[:], zr, start=True, stop=True))
            pe.wait_ge(S["wn_ready"], 1)
            o = take_bank(pe, "W1", 0)
            for r in range(2):
                last = t.matmul(o[0:NS, 16 * r:16 * r + 16], tb("FS")[:, NS * r:NS * r + NS], wn, start=True, stop=True)
            done(last)
            pe.wait_ge(S["w4_in"], 16)
            o = take_bank(pe, "W2", 0)
            done(t.matmul(o, tb("JT", NJ), in4, start=True, stop=True))
            pe.wait_ge(S["vv_ready"], 8)
            pe.wait_ge(S["w2_ready"], 1)
            for i in range(8):
                o = take_bank(pe, "OO", i)
                for m in range(2):
                    g = 2 * i + m
                    last = t.matmul(o[:, 256 * m:256 * m + 256], NM_[:, g, :], xt[:, 256 * g:256 * g + 256],
                                    start=True, stop=True)
                done(last)
            for i in range(8):
                pe.wait_ge(spec_in[i], 32)
            for i in range(8):
                o = take_bank(pe, "IV", i)
                done(t.matmul(o, tb("FT"), ct[:, 512 * i:512 * i + 512], start=True, stop=True))
            for i in range(8):
                pe.wait_ge(S["y_ready"], i // 2 + 1)
                o = take_bank(pe, "TY", i)
                for h in range(2):
                    for m in range(2):
                        b = 2 * i + m
                        last = t.transpose(o[:, 256 * h + 128 * m:256 * h + 128 * m + 128],
                                           kt[:, 256 * b + 128 * h:256 * b + 128 * h + 128], tb("I"))
                done(last)
            pe.wait_ge(S["am_ready"], 1)
            o = take_bank(pe, "AM1", 0)
            done(t.transpose(o[0:1, 0:128], am, tb("I")))
            pe.wait_ge(S["a1_ready"], 1)
            o = take_bank(pe, "AM2", 0)
            done(t.matmul(o[:, 0:1], ones[0:1, :], a2, start=True, stop=True))
            pe.wait_ge(S["winq_ready"], 2)
            for n in range(32):
                c, f = n // 8, n % 8
                if f == 0:
                    pe.wait_ge(S["yq_ready"], c + 1)
                o = take_bank(pe, "M1", n)
                first = True
                for k in range(2):
                    for part in (yhi, ylo):
                        last = t.matmul(o, winq[:, k, 128 * f:128 * f + 128], part[:, k, 512 * c:512 * c + 512],
                                        start=first, stop=(k == 1 and part is ylo))
                        first = False
                done(last)
            pe.wait_ge(S["hm_ready"], 1)
            o = take_bank(pe, "HM1", 0)
            done(t.transpose(o[0:1, 0:128], am, tb("I")))
            pe.wait_ge(S["ha_ready"], 1)
            o = take_bank(pe, "HM2", 0)
            done(t.matmul(o[:, 0:1], ones[0:1, :], a3, start=True, stop=True))
            for i in range(8):
                pe.wait_ge(S["hq_ready"], 4 * (i // 2) + 4)
                o = take_bank(pe, "M2", i)
                for m in range(2):
                    b = 2 * i + m
                    for f in range(8):
                        for part in range(2):
                            w = Hhi[:, f] if part == 0 else (Hlo5 if f < 4 else Hlo8)[:, f % 4]
                            last = t.matmul(o[:, 256 * m:256 * m + 256], w[:, 128 * b:128 * b + 128], woutq[:, f, :],
                                            start=(f == 0 and part == 0), stop=(f == 7 and part == 1))
                done(last)


def kernel(x, ctx_1024, L0_xattn_Wq, L0_xattn_bq, L0_xattn_Wk, L0_xattn_bk, L0_xattn_Wv, L0_xattn_bv,
           L0_xattn_Wo, L0_xattn_bo, L0_ffn_W_in, L0_ffn_b_in, L0_ffn_W_out, L0_ffn_b_out):
    import concourse.bacc as bacc
    from concourse.bass_utils import run_bass_kernel_spmd

    def cols(v):
        return np.asarray(v).reshape(-1, 128).T

    tab, at, indrow = shape_tables()
    arrays = {
        "x": x, "ctx_in": ctx_1024, "wq": L0_xattn_Wq, "wk": L0_xattn_Wk, "wvT": np.asarray(L0_xattn_Wv).T,
        "wo": L0_xattn_Wo, "winT": np.asarray(L0_ffn_W_in).T, "wout": L0_ffn_W_out,
        "cols": np.concatenate([cols(L0_xattn_bk), cols(L0_xattn_bq), cols(L0_xattn_bv), cols(L0_ffn_b_in)], 1),
        "rows": np.concatenate([np.asarray(L0_xattn_bo), np.asarray(L0_ffn_b_out)])[None],
        "tab": tab, "indrow": indrow,
    }
    arrays = {k: np.ascontiguousarray(v) for k, v in arrays.items()}
    nc = bacc.Bacc("TRN2", target_bir_lowering=False, num_devices=1)
    aps = {k: nc.dram_tensor(k + "_dram", v.shape, mybir.dt.from_np(v.dtype), kind="ExternalInput").ap()
           for k, v in arrays.items()}
    out = nc.dram_tensor("out_dram", (1, T, D), mybir.dt.float32, kind="ExternalOutput").ap()
    build(nc, out=out, at=at, **aps)
    r = run_bass_kernel_spmd(nc, [{k + "_dram": v for k, v in arrays.items()}], core_ids=[0])
    return r.results[0]["out_dram"]
```

```python
import concourse.bass as bass
from concourse import mybir
from contextlib import ExitStack
import numpy as np

T = 2048
TC = 1601
D = 256
FF = 1024
NA, NB = 128, 16
NS, NG, NJ = 64, 16, 4
NM = 32
TOPK = int(2 * np.log(T))
AF = TC // NB


def shape_tables():
    a, b = np.arange(NA), np.arange(NB)
    F = np.zeros((NA, NS, 2))
    for s in range(NS):
        F[:, s, 0] = np.cos(2 * np.pi * ((s * a) % NA) / NA)
        F[:, s, 1] = -np.sin(2 * np.pi * ((s * a) % NA) / NA)
    F[:, 0, 1] = 1.0 - 2.0 * (a % 2)
    U = np.zeros((NS, NM, NB, 2))
    V = np.zeros((NS, NM, NB, 2))
    sign = np.ones((NS, NM))
    for s in range(NS):
        for m in range(NM):
            k, part = m // 2, m % 2
            if s:
                f, w = s + NA * k, 2
            elif k == 0:
                f, w, part, src = (T // 2) * part, 1, 0, 0
            elif k < 8:
                f, w, src = NA * k, 2, 0
            else:
                f, w, src = NA // 2 + NA * (k - 8), 2, 1
            th = 2 * np.pi * ((f * b) % T) / T
            c, n = np.cos(th), -np.sin(th)
            if s:
                U[s, m, :, 0], U[s, m, :, 1] = (c, -n) if part == 0 else (n, c)
            else:
                U[s, m, :, src] = c if part == 0 else n
            V[s, m] = U[s, m] * w / T
            if part:
                sign[s, m] = 1.0 if f > T // 2 else -1.0
    P = V * (sign / D)[:, :, None, None]
    UR, UI, W = np.zeros_like(U), np.zeros_like(U), np.zeros_like(V)
    for m in range(NM):
        UR[:, m], UI[:, m] = U[:, m - m % 2], U[:, m - m % 2 + 1]
        W[:, m] = -V[:, m + 1] if m % 2 == 0 else V[:, m - 1]
    UR[0, 1], UI[0, 0:2], W[0, 0:2] = U[0, 1], 0, 0
    rows = [AF + 1 if x < TC - AF * NB else AF for x in range(NB)]
    ind = np.stack([F[0:rows[x]].sum(0) for x in range(NB)], 1)

    def by_row(x):
        return x.reshape(NG, NJ, NM, 32).transpose(1, 2, 0, 3).reshape(128, -1)

    out = {
        "F": F.reshape(NA, 128),
        "UT": U.reshape(NG, NJ, NM, 32).transpose(1, 3, 0, 2).reshape(128, -1),
        "IND": ind.reshape(NG, 128).T,
        "INDF": np.einsum("smbr,sbr->sm", U, ind).reshape(NG, 128).T,
        "U": by_row(U), "P": by_row(P),
        "FR": np.concatenate([F.reshape(NA, NG, NJ, 2).transpose(2, 1, 3, 0).reshape(NS, 256), np.zeros((64, 256))], 0),
        "J": np.kron(np.eye(NJ), np.ones((NM, NG))),
        "JT": np.concatenate([np.kron(np.eye(NJ), np.ones((NG, NM))), np.zeros((64, 128))], 0),
        "G": np.concatenate([np.tile(np.eye(NG), (NJ, 1)), np.zeros((64, NG))], 0),
        "UR": by_row(UR), "UI": by_row(UI), "V": by_row(V), "W": by_row(W),
        "FT": F.transpose(1, 2, 0).reshape(128, NA),
        "I": np.eye(128),
        "L": np.triu(np.ones((128, 128)), 1),
        "DK": np.concatenate([np.kron(np.eye(NB), np.ones((1, NB))), np.zeros((112, 256))], 0),
        "FS": F.reshape(NA, NG, NJ, 2).transpose(0, 3, 2, 1).reshape(NA, 128),
    }
    at, pos = {}, 0
    for k, x in out.items():
        at[k] = (pos, pos + x.shape[1])
        pos += x.shape[1]
    return np.concatenate(list(out.values()), 1).astype(np.float32), at


def build(nc, x, ctx_in, wqT, wkT, wvT, wo, winT, wout, cols, rows, tab, out, at):
    f32, bf16, f16 = mybir.dt.float32, mybir.dt.bfloat16, mybir.dt.float16
    ALU, ACT, AX = mybir.AluOpType, mybir.ActivationFunctionType, mybir.AxisListType
    MAGIC = 12582912.0
    TAKEN, PAST = -3.3e38, -3.0e38
    NCONST = tab.shape[1]
    es = ExitStack()
    with es:
        SL = 4096
        arena = es.enter_context(nc.sbuf_tensor("arena", [128, 9 * SL], f32))

        def slot(n, cols=SL, skip=0):
            return arena[:, n * SL + skip:n * SL + skip + cols]

        xs = slot(0)
        cx = slot(1)
        xh = slot(2)
        xt = slot(3)
        BU = slot(4, 2048).rearrange("p (g c) -> p g c", g=NG)
        NM_ = slot(4, 2048, 2048).rearrange("p (g c) -> p g c", g=NG)
        ct = slot(5)
        yn = slot(6)
        qt = slot(7)
        wraw = slot(8)
        H = arena[:, 1 * SL:5 * SL].rearrange("p (f t) -> p f t", f=8)
        Hhi = arena[:, 6 * SL:8 * SL].bitcast(f16).rearrange("p (f t) -> p f t", f=8)
        Hlo5 = slot(5).bitcast(f16).rearrange("p (f t) -> p f t", f=4)
        Hlo8 = slot(8).bitcast(f16).rearrange("p (f t) -> p f t", f=4)
        yhi = slot(5, 2048).bitcast(bf16).rearrange("p (h t) -> p h t", h=2)
        ylo = slot(5, 2048, 2048).bitcast(bf16).rearrange("p (h t) -> p h t", h=2)

        def sb(name, shape, dt=f32):
            return es.enter_context(nc.sbuf_tensor(name, shape, dt))

        tabs = sb("tabs", [128, NCONST])

        def tb(name, p=128):
            return tabs[0:p, at[name][0]:at[name][1]]

        def tb3(name):
            return tb(name).rearrange("p (g c) -> p g c", g=NG)

        wqT_s, wkT_s, wvT_s, wo_s = (slot(6, 512, 512 * i).rearrange("p (h n) -> p h n", h=2) for i in range(4))
        wqk, wvo = sb("wqk", [128, 2, D]), sb("wvo", [128, 2, D])
        wqbk = sb("wqbk", [128, D])
        bvo = sb("bvo", [128, D])
        bkb = slot(6, 256, 2048).rearrange("p (h n) -> p h n", h=2)
        bvb = slot(6, 256, 2304).rearrange("p (h n) -> p h n", h=2)
        winq = sb("winq", [128, 2, FF], bf16)
        woutq = sb("woutq", [128, 8, D], f16)
        colv = sb("colv", [128, 14])
        rowv = sb("rowv", [128, 2 * D])
        scr = sb("scr", [128, 4, 1024])
        scr16 = scr[:].rearrange("p n c -> p (n c)").bitcast(mybir.dt.int16)\
                      .rearrange("p (n c two) -> p n c two", n=4, two=2)[:, :, :, 0]
        winq_t = wraw[:, 0:1024].bitcast(bf16).rearrange("p (f d) -> p f d", f=8)
        wtmp = scr[:, 3, 0:D]
        gram = scr[:, 0, 0:512].rearrange("p (g c) -> p g c", g=NG)
        pr1 = scr[:, 0, 512:1024].rearrange("p (g c) -> p g c", g=NG)
        pr2 = scr[:, 1, 0:512].rearrange("p (g c) -> p g c", g=NG)
        own = scr[0:NS, 1, 512:1024]
        ownq = scr[0:NS, 3, 256:768]
        ins = sb("ins", [NS, NM])
        sm = sb("sm", [128, 704])
        sq = [0]

        def small(n, p=128):
            sq[0] += n
            return sm[0:p, sq[0] - n:sq[0]]

        eps, one, posM = small(1), small(1), small(1)
        bqk, bqbk, qb, qbs = small(2), small(1), small(16), small(16)
        st = small(96).rearrange("p (b k) -> p b k", b=NB)
        mv = small(32).rearrange("p (b k) -> p b k", b=NB)
        sd, rs, nt, nmr = small(16), small(16), small(16), small(16)
        warm = small(2)
        ab, mean, ex, wn, eq, pre, gone = (small(16) for _ in range(7))
        negmx, zr, rz, eqrow, neq = (small(1) for _ in range(5))
        m16 = small(16, NB)
        v16, exv, eqv = small(16), small(16), small(16)
        cand = scr[0:NB, 2, 0:256]
        left = scr[0:NB, 2, 256:256 + 128]
        left2 = scr[:, 2, 512:512 + 256]
        r1, r2 = small(16), small(16)
        wx, wm, wom = small(8), small(8), small(8)
        rf, hrf, wg, rwg = small(8), small(8), small(1), small(1)
        ss1, ss2 = small(8), small(8)
        ym, hm, am, yb, hb = small(4), small(17), small(1), small(1), small(1)
        ysc, hsc, sc1, sc2 = small(1), small(1), small(8), small(1)
        a1, a2, a3 = small(1, 1), small(1, 1), small(1, 1)
        ones = sb("ones", [128, 128])
        inv = sb("inv", [1, 128])
        identb = sb("identb", [128, 128], bf16)

        ps = es.enter_context(nc.psum_tensor("ps", [128, 8, 512], f32))

        def sem(name):
            return es.enter_context(nc.semaphore(name))

        names = ("ld_F ld_wqk ld_x ld_tab ld_wv ld_win ld_wout ld_col ld_row "
                 "pe dve_link act_link pool_const bu_ready xb_ready x2b_ready nz_ready "
                 "xh_a xh_d qt_ready wqk_ready qc_ready bkb_ready qb_ready ownq_ready qbs_ready wvo_ready bvo_ready bvb_ready gram_a gram_d ab_ready own_ready "
                 "ins_ready mean_ready cand_ready v16_ready ex_ready zr_ready eq_ready wn_ready "
                 "w1_ready vh_ready vv_ready w2_ready nm_ready os_a os_d x2_ready sd_ready "
                 "var_ready rs_ready y_a y_d yt_ready am_ready a1_ready ysc_ready wintq_ready winq_ready "
                 "wom_ready wg_ready rf_ready yu_ready yhi_ready yq_ready h_ready hm_ready ha_ready hsc_ready "
                 "yq_scale hu_a hu_d nm_a nm_c hp_ready hhi_ready hq_ready o_ready out_done ct_a ct_d xt_a xt_d bq_ready identb_ready").split()
        S = {n: sem(n) for n in names}
        ld_ctx = [sem(f"ld_ctx{i}") for i in range(5)]
        ld_xs = [sem(f"ld_x{i}") for i in range(4)]
        spec_in = [sem(f"spec_in{i}") for i in range(8)]
        spec_sw = [sem(f"spec_sw{i}") for i in range(4)]

        order = []
        order += [("CD", i) for i in range(8)] + [("GG", 0), ("SM", 0), ("WVO", 0), ("BVO", 0)]
        order += [("XD", i) for i in range(8)] + [("QP", i) for i in range(8)]
        order += [("QB1", 0), ("GR", 0), ("GR", 1), ("QB2", 0), ("GR", 2), ("GR", 3), ("UU", 0), ("WB", 0), ("WB", 1)]
        order += [("VP", 0), ("IN", 0), ("VP", 1), ("VP", 2), ("ME", 0), ("TM", 0), ("VP", 3), ("BC", 0)]
        order += [("VP", 4), ("EQ", 0), ("VP", 5), ("W1", 0), ("VP", 6), ("W2", 0), ("VP", 7)]
        order += [("VF", i) for i in range(8)]
        before_iv = len(order)
        order += [("OO", i) for i in range(8)] + [("IV", i) for i in range(8)]
        order += [("TY", i) for i in range(8)] + [("AM1", 0), ("AM2", 0)]
        order += [("M1", i) for i in range(8)] + [("WG1", 0)] + [("M1", i) for i in range(8, 16)] + [("WG2", 0)]
        order += [("M1", i) for i in range(16, 32)] + [("HM1", 0), ("HM2", 0)]
        order += [("M2", i) for i in range(16)]
        taken = order[:before_iv] + [("IV", i) for i in range(4)] + [("OO", i) for i in range(8)]
        taken += [("IV", i) for i in range(4, 8)] + order[before_iv + 16:]
        bank_no, previous, last_in = {}, {}, {}
        for n, u in enumerate(taken):
            k = {"IV": u[1], "OO": 4 + u[1] % 4}.get(u[0], n - before_iv)
            k += before_iv
            bank_no[u] = k % 8
            previous[u] = last_in.get(k % 8)
            last_in[k % 8] = u
        nth = {u: n for n, u in enumerate(order)}

        emptied = {
            "CD": lambda i: [(S["ct_a" if i % 2 == 0 else "ct_d"], i // 2 + 1)],
            "GG": lambda i: [(S["wqk_ready"], 1)],
            "SM": lambda i: [(S["qc_ready"], 1)],
            "QB1": lambda i: [(S["ownq_ready"], 1)],
            "QB2": lambda i: [(S["qbs_ready"], 1)],
            "XD": lambda i: [(S["xt_a" if i % 2 == 0 else "xt_d"], i // 2 + 1)],
            "QP": lambda i: [(S["qt_ready"], i + 1)],
            "GR": lambda i: [(S["gram_a"], i + 1), (S["gram_d"], i + 1)],
            "WVO": lambda i: [(S["wvo_ready"], 1)],
            "BVO": lambda i: [(S["bvo_ready"], 1)],
            "UU": lambda i: [(S["ab_ready"], 1)],
            "VP": lambda i: [(S["vh_ready"], i + 1)],
            "IN": lambda i: [(S["own_ready"], 1)],
            "ME": lambda i: [(S["mean_ready"], 1)],
            "VF": lambda i: [(S["vv_ready"], i + 1)],
            "WG1": lambda i: [(S["wg_ready"], 1)],
            "WG2": lambda i: [(S["rf_ready"], 1)],
            "WB": lambda i: [(S["winq_ready"], i + 1)],
            "TM": lambda i: [(S["cand_ready"], 1)],
            "BC": lambda i: [(S["v16_ready"], 1)],
            "EQ": lambda i: [(S["wn_ready"], 1)],
            "W1": lambda i: [(S["w1_ready"], 1)],
            "W2": lambda i: [(S["w2_ready"], 2)],
            "OO": lambda i: [(S["os_a" if i % 2 == 0 else "os_d"], i // 2 + 1)],
            "IV": lambda i: [(S["x2_ready"], i + 1)],
            "TY": lambda i: [(S["yt_ready"], i + 1)],
            "AM1": lambda i: [(S["a1_ready"], 1)],
            "AM2": lambda i: [(S["ysc_ready"], 1)],
            "M1": lambda i: [(S["h_ready"], i + 1)],
            "HM1": lambda i: [(S["ha_ready"], 1)],
            "HM2": lambda i: [(S["hsc_ready"], 1)],
            "M2": lambda i: [(S["o_ready"], i + 1)],
        }

        DVE_ROUNDS = (0, 3, 6, 9, 12, 14)

        def rounded_by(n):
            before = sum(k <= n for k in DVE_ROUNDS)
            return (S["hu_d"], before) if n in DVE_ROUNDS else (S["hu_a"], n + 1 - before)

        def bank(stage, i):
            return ps[:, bank_no[stage, i], :]

        def filled(eng, stage, i):
            eng.wait_ge(S["pe"], nth[stage, i] + 1)

        def take_bank(pe, stage, i):
            if previous[stage, i]:
                prev, k = previous[stage, i]
                for s, v in emptied[prev](k):
                    pe.wait_ge(s, v)
            return bank(stage, i)

        block = es.enter_context(nc.Block())

        @block.sync
        def _(sp):
            c3 = ctx_in[0, 0:AF * NB, :].rearrange("(a b) d -> a b d", b=NB)
            cs = cx.rearrange("p (b d) -> p b d", b=NB)
            sp.dma_start(tb("F"), tab[:, at["F"][0]:at["F"][1]]).then_inc(S["ld_F"], 16)
            sp.dma_start(cs[AF:AF + 1, 0, :], ctx_in[0, AF * NB:TC, :]).then_inc(ld_ctx[4], 16)
            for i in range(4):
                sp.dma_start(cs[0:AF, 4 * i:4 * i + 4, :], c3[:, 4 * i:4 * i + 4, :]).then_inc(ld_ctx[i], 16)
            for w_s, w in ((wqT_s, wqT), (wkT_s, wkT)):
                sp.dma_start(w_s, w.rearrange("(h p) n -> p h n", p=128)).then_inc(S["ld_wqk"], 16)
            sp.dma_start(colv[:], cols).then_inc(S["ld_col"], 16)
            x3 = x[0].rearrange("(a b) d -> a (b d)", b=NB)
            for i in range(4):
                sp.dma_start(xs[:, 1024 * i:1024 * i + 1024], x3[:, 1024 * i:1024 * i + 1024]).then_inc(ld_xs[i], 16)
            sp.dma_start(wvT_s, wvT.rearrange("(h p) n -> p h n", p=128)).then_inc(S["ld_wv"], 16)
            sp.dma_start(wo_s, wo.rearrange("(h p) n -> p h n", p=128)).then_inc(S["ld_wv"], 16)
            sp.dma_start(tabs[:, at["UT"][0]:NCONST], tab[:, at["UT"][0]:NCONST]).then_inc(S["ld_tab"], 16)
            sp.dma_start(rowv[:], rows[0:1, :].to_broadcast([128, 2 * D])).then_inc(S["ld_row"], 16)
            sp.dma_start(wraw[:, 0:2048].rearrange("p (f d) -> p f d", f=8),
                         winT.rearrange("(f p) d -> p f d", p=128)).then_inc(S["ld_win"], 16)
            sp.dma_start(wraw[:, 2048:4096].rearrange("p (f d) -> p f d", f=8),
                         wout.rearrange("(f p) d -> p f d", p=128)).then_inc(S["ld_wout"], 16)
            os3 = cx.rearrange("p (g c) -> p g c", g=NG)
            or3 = ct.rearrange("p (b c) -> p b c", b=NB)
            for i in range(8):
                sp.wait_ge(S["os_a" if i % 2 == 0 else "os_d"], i // 2 + 1)
                for g in (2 * i, 2 * i + 1) if i % 2 else (2 * i,):
                    sp.dma_start(or3[8 * g:8 * g + 8], os3[:, g, :]).then_inc(spec_in[i], 16)
            o3 = out[0].rearrange("(a b) d -> a (b d)", b=NB)
            for i in range(8):
                sp.wait_ge(S["o_ready"], 2 * i + 2)
                sp.dma_start(o3[:, 512 * i:512 * i + 512], xs[:, 512 * i:512 * i + 512]).then_inc(S["out_done"], 16)
            sp.wait_ge(S["out_done"], 8 * 16)

        @block.gpsimd
        def _(pool):
            g = nc.gpsimd
            g.memset(ones[:], 1.0)
            g.memset(one, 1.0)
            g.memset(inv[:], 1.0 / 32767.0)
            g.memset(posM, MAGIC)
            g.memset(eps, 1e-5)
            g.memset(BU, 0.0).then_inc(S["pool_const"], 1)
            g.memset(NM_, 0.0).then_inc(S["nz_ready"], 1)
            pool.wait_ge(S["nz_ready"], 1)
            pool.wait_ge(S["ld_tab"], 16)
            g.tensor_copy(identb[:], tb("I")).then_inc(S["identb_ready"], 1)
            pool.wait_ge(S["identb_ready"], 1)
            for j in range(NJ):
                q = slice(32 * j, 32 * j + 32)
                g.tensor_copy(BU[q, :, q], tb3("UT")[q]).then_inc(S["bu_ready"], 1)
                pool.wait_ge(S["bu_ready"], j + 1)
            pool.wait_ge(S["xh_a"], 2)
            pool.wait_ge(S["xh_d"], 2)
            pool.wait_ge(S["ld_row"], 16)
            x3 = xs.rearrange("p (b d) -> p b d", b=NB)
            g.tensor_tensor(x3, x3, rowv[:, 0:D].unsqueeze(1).to_broadcast([128, NB, D]), ALU.add).then_inc(S["xb_ready"], 1)
            pool.wait_ge(S["xb_ready"], 1)
            for i in range(0, 8, 2):
                pool.wait_ge(S["os_a"], i // 2 + 1)
                gg = 2 * i + 1
                g.dma_start(ct[8 * gg:8 * gg + 8, :].rearrange("p (b c) -> p b c", b=NB),
                            cx.rearrange("p (g c) -> p g c", g=NG)[:, gg, :]).then_inc(spec_sw[i // 2], 16)
            pool.wait_ge(S["yq_ready"], 4)
            g.tensor_tensor(x3, x3, rowv[:, D:2 * D].unsqueeze(1).to_broadcast([128, NB, D]), ALU.add).then_inc(S["x2b_ready"], 1)

        def spread(buf, h, bq):
            v = buf[:, h * 2048:(h + 1) * 2048].rearrange("p (s b r) -> p b s r", b=NB, r=2)
            return v[:, 4 * bq:4 * bq + 4]

        @block.scalar
        def _(act):
            a = nc.scalar
            linked = [0]

            def link(ins_):
                linked[0] += 1
                ins_.then_inc(S["act_link"], 1)
                act.wait_ge(S["act_link"], linked[0])

            act.wait_ge(S["pool_const"], 1)
            for i in range(0, 8, 2):
                filled(act, "CD", i)
                a.copy(spread(ct, 0, i // 2), bank("CD", i).rearrange("p (b s r) -> p b s r", b=4, r=2)).then_inc(S["ct_a"], 1)
            x3 = xs.rearrange("p (b d) -> p b d", b=NB)
            xh3 = xh.rearrange("p (b d) -> p b d", b=NB)
            y3 = yn.rearrange("p (b d) -> p b d", b=NB)
            act.wait_ge(S["var_ready"], 1)
            a.activation(sd[:, 0:8], mv[:, 0:8, 1], ACT.Sqrt, bias=eps).then_inc(S["sd_ready"], 1)
            filled(act, "GG", 0)
            a.copy(wqk[:].rearrange("p h n -> p (h n)"), bank("GG", 0)).then_inc(S["wqk_ready"], 1)
            filled(act, "SM", 0)
            link(a.copy(wqbk[:], bank("SM", 0)[:, 0:D]))
            link(a.copy(bqbk, bank("SM", 0)[:, D + 2:D + 3]))
            a.mul(bqk, bank("SM", 0)[:, D:D + 2], float(NA)).then_inc(S["qc_ready"], 1)
            filled(act, "WVO", 0)
            a.copy(wvo[:].rearrange("p h n -> p (h n)"), bank("WVO", 0)).then_inc(S["wvo_ready"], 1)
            filled(act, "BVO", 0)
            a.copy(bvo[:], bank("BVO", 0)[:, 0:D]).then_inc(S["bvo_ready"], 1)
            for k in range(2):
                if k == 1:
                    act.wait_ge(S["var_ready"], 2)
                    a.activation(sd[:, 8:16], mv[:, 8:16, 1], ACT.Sqrt, bias=eps).then_inc(S["sd_ready"], 1)
                act.wait_ge(S["rs_ready"], k + 1)
                for b in range(8 * k + 4, 8 * k + 8):
                    ins_ = a.activation(xh3[:, b, :], x3[:, b, :], ACT.Identity, bias=nmr[:, b:b + 1], scale=rs[:, b:b + 1])
                ins_.then_inc(S["xh_a"], 1)
            for i in range(0, 8, 2):
                filled(act, "XD", i)
                a.copy(spread(xt, 0, i // 2), bank("XD", i).rearrange("p (b s r) -> p b s r", b=4, r=2)).then_inc(S["xt_a"], 1)
            act.wait_ge(S["qc_ready"], 1)
            for i in range(8):
                h, c = i // 4, i % 4
                filled(act, "QP", i)
                dst = qt[:, h * 2048 + c * 512:h * 2048 + c * 512 + 512]
                src = bank("QP", i)
                if c == 0:
                    a.activation(dst[:, 0:32:2], src[:, 0:32:2], ACT.Identity, bias=bqk[:, h:h + 1])
                    a.copy(dst[:, 1:32:2], src[:, 1:32:2])
                    a.copy(dst[:, 32:512], src[:, 32:512]).then_inc(S["qt_ready"], 1)
                else:
                    a.copy(dst, src).then_inc(S["qt_ready"], 1)
            for i in range(4):
                filled(act, "GR", i)
                for j in (0, 1):
                    q = slice(32 * j, 32 * j + 32)
                    ins_ = a.copy(gram[q, 4 * i:4 * i + 4, :],
                                  bank("GR", i).rearrange("p (g c) -> p g c", g=4)[q, :, q])
                ins_.then_inc(S["gram_a"], 1)
            for i in range(2):
                filled(act, "WB", i)
                a.copy(winq[:, i, :], bank("WB", i).bitcast(bf16)).then_inc(S["winq_ready"], 1)
            a.activation(warm[:, 0:1], one, ACT.Exp)
            act.wait_ge(S["v16_ready"], 1)
            link(a.mul(negmx, v16[:, 0:1], -1.0))
            a.activation(exv[:, 0:TOPK], v16[:, 0:TOPK], ACT.Exp, bias=negmx, accum_out=zr)
            a.activation(ex, mean, ACT.Exp, bias=negmx).then_inc(S["ex_ready"], 1)
            def vcopy(*units):
                for i in units:
                    filled(act, "VF", i)
                    a.copy(xt[:, 512 * i:512 * i + 512], bank("VF", i)).then_inc(S["vv_ready"], 1)

            def place(h):
                act.wait_ge(S["nm_c"], h + 1)
                gs = slice(8 * h, 8 * h + 8)
                for j in (0, 1):
                    q = slice(32 * j, 32 * j + 32)
                    ins_ = a.copy(NM_[q, gs, q].rearrange("p g (r b) -> p g b r", r=2),
                                  pr1[q, gs].rearrange("p g (b r) -> p g b r", r=2))
                ins_.then_inc(S["nm_a"], 1)

            vcopy(0, 1, 2)
            place(0)
            vcopy(3, 4, 5)
            place(1)
            vcopy(6, 7)
            for i in range(0, 8, 2):
                filled(act, "OO", i)
                a.copy(cx[:, 512 * i:512 * i + 512], bank("OO", i)).then_inc(S["os_a"], 1)

            def transposed(k):
                for i in (2 * k, 2 * k + 1):
                    filled(act, "TY", i)
                    a.copy(qt.rearrange("p (h t) -> p h t", h=2)[:, :, 256 * i:256 * i + 256],
                           bank("TY", i).rearrange("p (h t) -> p h t", h=2)).then_inc(S["yt_ready"], 1)

            def normalise(k):
                act.wait_ge(S["rs_ready"], k + 3)
                for b in (4 * k, 4 * k + 1):
                    ins_ = a.activation(y3[:, b, :], x3[:, b, :], ACT.Identity, bias=nmr[:, b:b + 1], scale=rs[:, b:b + 1])
                ins_.then_inc(S["y_a"], 1)

            def x2_copy(*units):
                for i in units:
                    filled(act, "IV", i)
                    a.copy(xs[:, 512 * i:512 * i + 512], bank("IV", i)).then_inc(S["x2_ready"], 1)

            def deviation(k):
                act.wait_ge(S["var_ready"], k + 3)
                a.activation(sd[:, 4 * k:4 * k + 4], mv[:, 4 * k:4 * k + 4, 1], ACT.Sqrt, bias=eps).then_inc(S["sd_ready"], 1)

            x2_copy(0, 1, 2, 3)
            deviation(0)
            x2_copy(4, 5)
            deviation(1)
            normalise(0)
            x2_copy(6, 7)
            deviation(2)
            normalise(1)
            transposed(0)
            deviation(3)
            normalise(2)
            transposed(1)
            normalise(3)
            transposed(2)
            transposed(3)
            a.activation(warm[:, 1:2], one, ACT.Gelu)
            act.wait_ge(S["yq_scale"], 1)
            act.wait_ge(S["yt_ready"], 8)
            yt3 = qt.rearrange("p (h t) -> p h t", h=2)
            for c in range(4):
                a.mul(yhi[:, :, 512 * c:512 * c + 512], yt3[:, :, 512 * c:512 * c + 512], ysc)\
                 .then_inc(S["yhi_ready"], 1)
            act.wait_ge(S["ysc_ready"], 1)
            for n in range(32):
                c, f = n // 8, n % 8
                filled(act, "M1", n)
                a.activation(H[:, f, 512 * c:512 * c + 512], bank("M1", n), ACT.Gelu,
                             bias=colv[:, 6 + f:7 + f], scale=sc1[:, f:f + 1]).then_inc(S["h_ready"], 1)
            act.wait_ge(S["hsc_ready"], 1)

            def rounded(n):
                c, f = n // 4, 2 * (n % 4)
                if n >= 4:
                    act.wait_ge(S["hq_ready"], n - 3)
                a.activation(scr[:, n % 4, :].rearrange("p (f t) -> p f t", f=2), H[:, f:f + 2, 512 * c:512 * c + 512],
                             ACT.Identity, bias=posM, scale=hsc).then_inc(S["hu_a"], 1)

            def high(n):
                c, f = n // 4, 2 * (n % 4)
                for k in range(2):
                    ins_ = a.mul(Hhi[:, f + k, 512 * c:512 * c + 512], H[:, f + k, 512 * c:512 * c + 512],
                                 hrf[:, f + k:f + k + 1])
                ins_.then_inc(S["hhi_ready"], 1)

            for n in range(16):
                high(n)
                if n < 15 and n + 1 not in DVE_ROUNDS:
                    rounded(n + 1)

        @block.vector
        def _(dve):
            v = nc.vector
            linked = [0]

            def link(ins_):
                linked[0] += 1
                ins_.then_inc(S["dve_link"], 1)
                dve.wait_ge(S["dve_link"], linked[0])

            x3 = xs.rearrange("p (b d) -> p b d", b=NB)
            xh3 = xh.rearrange("p (b d) -> p b d", b=NB)
            def vproj(i):
                filled(dve, "VP", i)
                for k in range(2):
                    gg = 2 * i + k
                    ins_ = v.scalar_tensor_tensor(out=xh[:, 256 * gg:256 * gg + 256], in0=bvo[:],
                                                  scalar=tb("IND")[:, gg:gg + 1],
                                                  in1=bank("VP", i)[:, 256 * k:256 * k + 256],
                                                  op0=ALU.mult, op1=ALU.add)
                ins_.then_inc(S["vh_ready"], 1)

            def spread_bins(dst, src):
                return v.tensor_tensor(dst.rearrange("s (g b r) -> s g b r", g=NG, r=2),
                                       src[0:NS, 0:NM].rearrange("s (r b) -> s b r", r=2).unsqueeze(1).to_broadcast([NS, NG, NB, 2]),
                                       tb("G", NS).unsqueeze(2).unsqueeze(3).to_broadcast([NS, NG, NB, 2]), ALU.mult)

            def newton(lo, hi):
                r, n_, w = rs[:, lo:hi], nt[:, lo:hi], mv[:, lo:hi, 1]
                link(v.reciprocal(r, sd[:, lo:hi]))
                link(v.scalar_tensor_tensor(out=n_, in0=w, scalar=1e-5, in1=r, op0=ALU.add, op1=ALU.mult))
                link(v.scalar_tensor_tensor(out=n_, in0=n_, scalar=-0.5, in1=r, op0=ALU.mult, op1=ALU.mult))
                link(v.scalar_tensor_tensor(out=r, in0=n_, scalar=1.5, in1=r, op0=ALU.add, op1=ALU.mult))
                v.scalar_tensor_tensor(out=nmr[:, lo:hi], in0=mv[:, lo:hi, 0], scalar=-1.0, in1=r,
                                       op0=ALU.mult, op1=ALU.mult).then_inc(S["rs_ready"], 1)

            def normalise_x(k):
                dve.wait_ge(S["sd_ready"], k + 1)
                newton(8 * k, 8 * k + 8)
                for b in range(8 * k, 8 * k + 4):
                    ins_ = v.tensor_scalar(xh3[:, b, :], x3[:, b, :], mv[:, b, 0:1], rs[:, b:b + 1], ALU.subtract, ALU.mult)
                ins_.then_inc(S["xh_d"], 1)

            dve.wait_ge(S["ld_col"], 16)
            v.tensor_copy(bkb, colv[:, 0:2].unsqueeze(2).to_broadcast([128, 2, 128])).then_inc(S["bkb_ready"], 1)
            v.tensor_copy(bvb, colv[:, 4:6].unsqueeze(2).to_broadcast([128, 2, 128])).then_inc(S["bvb_ready"], 1)
            for i in range(4):
                filled(dve, "CD", 2 * i + 1)
                v.tensor_copy(spread(ct, 1, i), bank("CD", 2 * i + 1).rearrange("p (b s r) -> p b s r", b=4, r=2))\
                 .then_inc(S["ct_d"], 1)
                dve.wait_ge(ld_xs[i], 16)
                for b in range(4 * i, 4 * i + 4):
                    ins_ = v.bn_stats(st[:, b, :], x3[:, b, :])
                if i % 2:
                    link(ins_)
                    for b in range(4 * i - 4, 4 * i + 4):
                        ins_ = v.bn_aggr(mv[:, b, :], st[:, b, :])
                    ins_.then_inc(S["var_ready"], 1)
            dve.wait_ge(S["var_ready"], 2)
            normalise_x(0)
            normalise_x(1)
            for k in range(1, 8, 2):
                filled(dve, "XD", k)
                v.tensor_copy(spread(xt, 1, k // 2), bank("XD", k).rearrange("p (b s r) -> p b s r", b=4, r=2))\
                 .then_inc(S["xt_d"], 1)
            dve.wait_ge(S["qc_ready"], 1)
            dve.wait_ge(S["xh_a"], 2)
            for b in range(NB):
                ins_ = v.tensor_tensor_reduce(out=cx[:, 256 * b:256 * b + 256], in0=xh3[:, b, :], in1=wqbk[:], scale=1.0, scalar=0.0,
                                              op0=ALU.mult, op1=ALU.add, accum_out=qb[:, b:b + 1])
            link(ins_)
            v.tensor_scalar(qb, qb, bqbk, None, ALU.add).then_inc(S["qb_ready"], 1)
            dve.wait_ge(S["ld_win"], 16)
            win3 = wraw[:, 0:2048].rearrange("p (f d) -> p f d", f=8)
            wou3 = wraw[:, 2048:4096].rearrange("p (f d) -> p f d", f=8)
            link(v.tensor_reduce(wx, win3, AX.X, ALU.max, apply_absolute_value=True))
            link(v.tensor_scalar(wx, wx, 1e-8, None, ALU.max))
            link(v.reciprocal(ss1, wx))
            link(v.tensor_scalar(ss1, ss1, 127.0, None, ALU.mult))
            for f in range(8):
                link(v.tensor_scalar(wtmp, win3[:, f, :], ss1[:, f:f + 1], MAGIC, ALU.mult, ALU.add))
                link(v.tensor_scalar(winq_t[:, f, :], wtmp, MAGIC, None, ALU.subtract))
            dve.wait_ge(S["ld_tab"], 16)
            filled(dve, "QB1", 0)
            spread_bins(ownq, bank("QB1", 0)).then_inc(S["ownq_ready"], 1)
            for i in range(4):
                if i == 2:
                    filled(dve, "QB2", 0)
                    link(v.tensor_tensor(pr1, bank("QB2", 0).rearrange("p (g c) -> p g c", g=NG), tb3("U"), ALU.mult))
                    link(v.tensor_reduce(qbs, pr1, AX.X, ALU.add))
                    v.tensor_tensor(qbs, qbs, tb("INDF"), ALU.mult).then_inc(S["qbs_ready"], 1)
                filled(dve, "GR", i)
                for j in (2, 3):
                    q = slice(32 * j, 32 * j + 32)
                    ins_ = v.tensor_copy(gram[q, 4 * i:4 * i + 4, :],
                                         bank("GR", i).rearrange("p (g c) -> p g c", g=4)[q, :, q])
                ins_.then_inc(S["gram_d"], 1)
            filled(dve, "UU", 0)
            link(v.tensor_tensor(pr1, bank("UU", 0).rearrange("p (g c) -> p g c", g=NG), tb3("U"), ALU.mult))
            link(v.tensor_reduce(ab, pr1, AX.X, ALU.add))
            dve.wait_ge(S["qbs_ready"], 1)
            link(v.tensor_tensor(ab, ab, qbs, ALU.add))
            v.tensor_tensor(pr2, tb3("P"), ab.unsqueeze(2).to_broadcast([128, NG, 32]), ALU.mult)\
             .then_inc(S["ab_ready"], 1)

            dve.wait_ge(S["bvo_ready"], 1)
            vproj(0)
            filled(dve, "IN", 0)
            link(v.tensor_tensor(own.rearrange("s (g c) -> s g c", g=NG), bank("IN", 0)[0:NS, :].rearrange("s (g c) -> s g c", g=NG),
                                 tb("G", NS).unsqueeze(2).to_broadcast([NS, NG, NM]), ALU.mult))
            v.tensor_reduce(ins[:], own.rearrange("s (g c) -> s c g", g=NG), AX.X, ALU.add).then_inc(S["own_ready"], 1)
            vproj(1)
            vproj(2)
            filled(dve, "ME", 0)
            v.tensor_copy(mean, bank("ME", 0)[:, 0:NB]).then_inc(S["mean_ready"], 1)
            filled(dve, "TM", 0)
            tm = bank("TM", 0)[0:NB, 0:128]
            link(v.max(m16[:, 0:8], tm))
            link(v.match_replace(left, m16[:, 0:8], tm, TAKEN))
            link(v.max(m16[:, 8:16], left))
            v.tensor_tensor(cand.rearrange("p (k i) -> p k i", k=NB), m16.unsqueeze(1).to_broadcast([NB, NB, NB]),
                            tb("DK", NB).rearrange("p (k i) -> p k i", k=NB), ALU.mult).then_inc(S["cand_ready"], 1)
            vproj(3)
            filled(dve, "BC", 0)
            bc = bank("BC", 0)[:, 0:256]
            link(v.max(v16[:, 0:8], bc))
            link(v.match_replace(left2, v16[:, 0:8], bc, TAKEN))
            v.max(v16[:, 8:16], left2).then_inc(S["v16_ready"], 1)
            dve.wait_ge(S["v16_ready"], 1)
            last_v = v16[:, TOPK - 1:TOPK]
            link(v.tensor_scalar(eq, mean, last_v, None, ALU.is_equal))
            v.reduce_sum(eqrow, eq, AX.X).then_inc(S["eq_ready"], 1)
            link(v.tensor_scalar(eqv[:, 0:TOPK], v16[:, 0:TOPK], last_v, None, ALU.is_equal))
            link(v.reduce_sum(neq, eqv[:, 0:TOPK], AX.X))
            vproj(4)
            dve.wait_ge(S["ex_ready"], 1)
            link(v.reciprocal(rz, zr))
            filled(dve, "EQ", 0)
            link(v.tensor_tensor_scan(pre, ones[:, 0:NB], eq, bank("EQ", 0)[:, 0:1], ALU.mult, ALU.add))
            link(v.scalar_tensor_tensor(out=gone, in0=pre, scalar=neq, in1=eq, op0=ALU.is_le, op1=ALU.mult))
            link(v.scalar_tensor_tensor(out=gone, in0=mean, scalar=last_v, in1=gone, op0=ALU.is_gt, op1=ALU.add))
            v.scalar_tensor_tensor(out=wn, in0=gone, scalar=rz, in1=ex, op0=ALU.mult, op1=ALU.mult)\
             .then_inc(S["wn_ready"], 1)
            vproj(5)
            filled(dve, "W1", 0)
            spread_bins(own, bank("W1", 0)).then_inc(S["w1_ready"], 1)
            vproj(6)
            filled(dve, "W2", 0)
            w2 = bank("W2", 0).rearrange("p (g c) -> p g c", g=NG)
            for h in range(2):
                gs = slice(8 * h, 8 * h + 8)
                v.tensor_tensor(pr1[:, gs], w2[:, gs], tb3("UR")[:, gs], ALU.mult)
                ins_ = v.tensor_tensor(pr2[:, gs], w2[:, gs], tb3("UI")[:, gs], ALU.mult)
                ins_.then_inc(S["w2_ready"], 1)
                dve.wait_ge(S["w2_ready"], h + 1)
                v.tensor_reduce(r1[:, gs], pr1[:, gs], AX.X, ALU.add)
                link(v.tensor_reduce(r2[:, gs], pr2[:, gs], AX.X, ALU.add))
                v.tensor_tensor(pr1[:, gs], tb3("V")[:, gs], r1[:, gs].unsqueeze(2).to_broadcast([128, 8, 32]), ALU.mult)
                link(v.tensor_tensor(pr2[:, gs], tb3("W")[:, gs], r2[:, gs].unsqueeze(2).to_broadcast([128, 8, 32]), ALU.mult))
                v.tensor_tensor(pr1[:, gs], pr1[:, gs], pr2[:, gs], ALU.add).then_inc(S["nm_c"], 1)
                dve.wait_ge(S["nm_c"], h + 1)
                for j in (2, 3):
                    q = slice(32 * j, 32 * j + 32)
                    ins_ = v.tensor_copy(NM_[q, gs, q].rearrange("p g (r b) -> p g b r", r=2),
                                         pr1[q, gs].rearrange("p g (b r) -> p g b r", r=2))
                ins_.then_inc(S["nm_ready"], 1)
                if h == 0:
                    vproj(7)
            dve.wait_ge(S["ld_wout"], 16)
            link(v.tensor_reduce(wom, wou3, AX.X, ALU.max, apply_absolute_value=True))
            link(v.tensor_scalar(wom, wom, 1e-8, None, ALU.max))
            v.tensor_reduce(wg, wom, AX.X, ALU.max).then_inc(S["wom_ready"], 1)
            link(v.reciprocal(ss2, wom))
            link(v.tensor_scalar(ss2, ss2, 127.0, None, ALU.mult))
            for f in range(8):
                link(v.tensor_scalar(wtmp, wou3[:, f, :], ss2[:, f:f + 1], MAGIC, ALU.mult, ALU.add))
                link(v.tensor_scalar(woutq[:, f, :], wtmp, MAGIC, None, ALU.subtract))
                if f % 2:
                    filled(dve, "OO", f)
                    v.tensor_copy(cx[:, 512 * f:512 * f + 512], bank("OO", f)).then_inc(S["os_d"], 1)
            y3 = yn.rearrange("p (b d) -> p b d", b=NB)

            def statistics(k):
                for i in (2 * k, 2 * k + 1):
                    dve.wait_ge(S["x2_ready"], i + 1)
                    for b in (2 * i, 2 * i + 1):
                        ins_ = v.bn_stats(st[:, b, :], x3[:, b, :])
                link(ins_)
                for b in range(4 * k, 4 * k + 4):
                    ins_ = v.bn_aggr(mv[:, b, :], st[:, b, :])
                ins_.then_inc(S["var_ready"], 1)

            def normalise(k):
                dve.wait_ge(S["sd_ready"], 3 + k)
                newton(4 * k, 4 * k + 4)
                for b in (4 * k + 2, 4 * k + 3):
                    ins_ = v.tensor_scalar(y3[:, b, :], x3[:, b, :], mv[:, b, 0:1], rs[:, b:b + 1], ALU.subtract, ALU.mult)
                ins_.then_inc(S["y_d"], 1)

            def largest(k):
                dve.wait_ge(S["y_a"], k + 1)
                dve.wait_ge(S["y_d"], k + 1)
                return v.tensor_reduce(ym[:, k:k + 1], y3[:, 4 * k:4 * k + 4, :].rearrange("p b d -> p (b d)"), AX.X,
                                       ALU.max, apply_absolute_value=True)

            for k in range(4):
                statistics(k)
                if k >= 1:
                    normalise(k - 1)
                if k >= 2:
                    largest(k - 2)
            normalise(3)
            largest(2)
            ins_ = largest(3)
            link(ins_)
            v.reduce_max(am, ym, AX.X).then_inc(S["am_ready"], 1)
            filled(dve, "AM1", 0)
            v.reduce_max(a2, bank("AM1", 0)[0:1, 0:128], AX.X).then_inc(S["a1_ready"], 1)
            filled(dve, "AM2", 0)
            link(v.tensor_scalar(yb, bank("AM2", 0)[:, 0:1], 1e-8 / 32767.0, None, ALU.max))
            v.reciprocal(ysc, yb).then_inc(S["yq_scale"], 1)
            dve.wait_ge(S["yq_scale"], 1)
            dve.wait_ge(S["yt_ready"], 8)
            yt3 = qt.rearrange("p (h t) -> p h t", h=2)

            def y_round(c):
                v.tensor_scalar(scr[:, c, :].rearrange("p (h t) -> p h t", h=2), yt3[:, :, 512 * c:512 * c + 512],
                                ysc, MAGIC, ALU.mult, ALU.add).then_inc(S["yu_ready"], 1)

            y_round(0)
            link(v.tensor_scalar(yb, yb, 1.0 / 127.0, None, ALU.mult))
            v.tensor_scalar(sc1, wx, yb, None, ALU.mult).then_inc(S["ysc_ready"], 1)
            for c in range(4):
                if c < 3:
                    y_round(c + 1)
                dve.wait_ge(S["yhi_ready"], c + 1)
                dve.wait_ge(S["yu_ready"], c + 1)
                v.tensor_tensor(ylo[:, :, 512 * c:512 * c + 512], scr16[:, c, :].rearrange("p (h t) -> p h t", h=2),
                                yhi[:, :, 512 * c:512 * c + 512], ALU.subtract).then_inc(S["yq_ready"], 1)
            for n in range(16):
                c, f = n // 4, 2 * (n % 4)
                if n == 4:
                    filled(dve, "WG1", 0)
                    v.reduce_max(a1, bank("WG1", 0)[0:1, 0:128], AX.X).then_inc(S["wg_ready"], 1)
                if n == 8:
                    filled(dve, "WG2", 0)
                    link(v.tensor_copy(wg, bank("WG2", 0)[:, 0:1]))
                    link(v.reciprocal(rwg, wg))
                    v.tensor_scalar(rf, wom, rwg, None, ALU.mult).then_inc(S["rf_ready"], 1)
                for k in ((0, 2),) if n < 15 else ((0, 1), (1, 1)):
                    dve.wait_ge(S["h_ready"], 2 * n + k[0] + k[1])
                    ins_ = v.tensor_reduce(hm[:, n + k[0]:n + k[0] + 1], H[:, f + k[0]:f + k[0] + k[1], 512 * c:512 * c + 512],
                                           AX.XY, ALU.max, apply_absolute_value=True)
            link(ins_)
            v.reduce_max(am, hm, AX.X).then_inc(S["hm_ready"], 1)
            filled(dve, "HM1", 0)
            v.reduce_max(a3, bank("HM1", 0)[0:1, 0:128], AX.X).then_inc(S["ha_ready"], 1)
            filled(dve, "HM2", 0)
            link(v.tensor_scalar(hb, bank("HM2", 0)[:, 0:1], 1e-8 / 32767.0, None, ALU.max))
            link(v.reciprocal(hsc, hb))
            v.tensor_scalar(hrf, rf, hsc, None, ALU.mult).then_inc(S["hsc_ready"], 1)

            def rounded(n):
                c, f = n // 4, 2 * (n % 4)
                if n >= 4:
                    dve.wait_ge(S["hq_ready"], n - 3)
                v.tensor_scalar(scr[:, n % 4, :].rearrange("p (f t) -> p f t", f=2), H[:, f:f + 2, 512 * c:512 * c + 512],
                                hsc, MAGIC, ALU.mult, ALU.add).then_inc(S["hu_d"], 1)

            def low(n):
                c, f = n // 4, 2 * (n % 4)
                dve.wait_ge(S["hhi_ready"], n + 1)
                dve.wait_ge(*rounded_by(n))
                part = (Hlo5 if f < 4 else Hlo8)[:, f % 4:f % 4 + 2, 512 * c:512 * c + 512]
                for k in range(2):
                    ins_ = v.scalar_tensor_tensor(out=part[:, k, :], in0=scr16[:, n % 4, 512 * k:512 * k + 512],
                                                  scalar=rf[:, f + k:f + k + 1], in1=Hhi[:, f + k, 512 * c:512 * c + 512],
                                                  op0=ALU.mult, op1=ALU.subtract)
                ins_.then_inc(S["hq_ready"], 1)

            def final(b):
                filled(dve, "M2", b)
                v.scalar_tensor_tensor(out=xs[:, 256 * b:256 * b + 256], in0=bank("M2", b)[:, 0:256], scalar=sc2,
                                       in1=xs[:, 256 * b:256 * b + 256], op0=ALU.mult, op1=ALU.add)\
                 .then_inc(S["o_ready"], 1)

            rounded(0)
            link(v.tensor_scalar(sc2, hb, 1.0 / 127.0, None, ALU.mult))
            link(v.tensor_scalar(sc2, sc2, wg, None, ALU.mult))
            dve.wait_ge(S["x2b_ready"], 1)
            for n in range(16):
                if n + 1 in DVE_ROUNDS:
                    rounded(n + 1)
                low(n)
                if n >= 6 and n % 4 >= 2:
                    b = 4 * (n // 4 - 1) + 2 * (n % 4 - 2)
                    final(b)
                    final(b + 1)
            for b in range(12, 16):
                final(b)

        @block.tensor
        def _(pe):
            t = nc.tensor
            F = tb("F")

            def done(ins_):
                ins_.then_inc(S["pe"], 1)

            pe.wait_ge(S["ld_F"], 16)
            pe.wait_ge(ld_ctx[4], 16)
            for i in range(8):
                bq, h = i // 2, i % 2
                if h == 0:
                    pe.wait_ge(ld_ctx[bq], 16)
                o = take_bank(pe, "CD", i)
                for k in range(4):
                    b = 4 * bq + k
                    n = AF + 1 if b < TC - AF * NB else AF
                    last = t.matmul(o[:, 128 * k:128 * k + 128], cx[0:n, 256 * b + 128 * h:256 * b + 128 * h + 128],
                                    F[0:n, :], start=True, stop=True)
                done(last)
            pe.wait_ge(S["ld_wqk"], 32)
            o = take_bank(pe, "GG", 0)
            for h in range(2):
                for k in range(2):
                    last = t.matmul(o[:, 256 * h:256 * h + 256], wqT_s[:, k, 128 * h:128 * h + 128], wkT_s[:, k, :],
                                    start=(k == 0), stop=(k == 1))
            done(last)
            pe.wait_ge(S["bkb_ready"], 1)
            pe.wait_ge(S["ld_col"], 16)
            o = take_bank(pe, "SM", 0)
            for k in range(2):
                t.matmul(o[:, 0:D], bkb[:, k, :], wqT_s[:, k, :], start=(k == 0), stop=(k == 1))
            for h in range(2):
                for k in range(2):
                    t.matmul(o[:, D + h:D + h + 1], wkT_s[:, k, 128 * h:128 * h + 128], colv[:, 2 + k:3 + k],
                             start=(k == 0), stop=(k == 1))
            for k in range(2):
                last = t.matmul(o[:, D + 2:D + 3], bkb[:, k, :], colv[:, 2 + k:3 + k], start=(k == 0), stop=(k == 1))
            done(last)
            pe.wait_ge(S["ld_wv"], 32)
            o = take_bank(pe, "WVO", 0)
            for h in range(2):
                for k in range(2):
                    last = t.matmul(o[:, 256 * h:256 * h + 256], wvT_s[:, k, 128 * h:128 * h + 128], wo_s[:, k, :],
                                    start=(k == 0), stop=(k == 1))
            done(last)
            pe.wait_ge(S["bvb_ready"], 1)
            o = take_bank(pe, "BVO", 0)
            for k in range(2):
                last = t.matmul(o[:, 0:D], bvb[:, k, :], wo_s[:, k, :], start=(k == 0), stop=(k == 1))
            done(last)

            def vproj(i):
                o = take_bank(pe, "VP", i)
                for m in range(2):
                    for k in range(2):
                        c0 = 2048 * k + 128 * (2 * i + m)
                        last = t.matmul(o[:, 256 * m:256 * m + 256], ct[:, c0:c0 + 128], wvo[:, k, :],
                                        start=(k == 0), stop=(k == 1))
                done(last)

            pe.wait_ge(S["ct_a"], 4)
            pe.wait_ge(S["ct_d"], 4)
            pe.wait_ge(S["wvo_ready"], 1)
            for i in range(8):
                bq, h = i // 2, i % 2
                if h == 0:
                    pe.wait_ge(S["xh_a" if bq % 2 else "xh_d"], bq // 2 + 1)
                o = take_bank(pe, "XD", i)
                for k in range(4):
                    b = 4 * bq + k
                    last = t.matmul(o[:, 128 * k:128 * k + 128], xh[:, 256 * b + 128 * h:256 * b + 128 * h + 128],
                                    F, start=True, stop=True)
                done(last)
            pe.wait_ge(S["wqk_ready"], 1)
            pe.wait_ge(S["xt_a"], 4)
            pe.wait_ge(S["xt_d"], 4)
            for i in range(8):
                h, c = i // 4, i % 4
                o = take_bank(pe, "QP", i)
                for k in range(2):
                    last = t.matmul(o, wqk[:, k, 128 * h:128 * h + 128], xt[:, 2048 * k + 512 * c:2048 * k + 512 * c + 512],
                                    start=(k == 0), stop=(k == 1))
                done(last)
            pe.wait_ge(S["ld_tab"], 16)
            pe.wait_ge(S["qb_ready"], 1)
            o = take_bank(pe, "QB1", 0)
            for r in range(2):
                last = t.matmul(o[0:NS, 16 * r:16 * r + 16], tb("FS")[:, NS * r:NS * r + NS], qb, start=True, stop=True)
            done(last)
            pe.wait_ge(S["qt_ready"], 8)
            def gramian(i):
                o = take_bank(pe, "GR", i)
                for m in range(4):
                    g = 4 * i + m
                    for k in range(2):
                        c0 = 2048 * k + 128 * g
                        last = t.matmul(o[:, 128 * m:128 * m + 128], ct[:, c0:c0 + 128], qt[:, c0:c0 + 128],
                                        start=(k == 0), stop=(k == 1))
                done(last)

            def second_step(i):
                pe.wait_ge(S["gram_a"], i + 1)
                pe.wait_ge(S["gram_d"], i + 1)
                for g in range(4 * i, 4 * i + 4):
                    last = t.matmul(bank("UU", 0)[:, 32 * g:32 * g + 32], BU[:, g, :], gram[:, g, :], start=True, stop=True)
                return last

            gramian(0)
            gramian(1)
            pe.wait_ge(S["ownq_ready"], 1)
            o = take_bank(pe, "QB2", 0)
            done(t.matmul(o, tb("JT", NS), ownq, start=True, stop=True))
            pe.wait_ge(S["bu_ready"], NJ)
            take_bank(pe, "UU", 0)
            second_step(0)
            gramian(2)
            second_step(1)
            gramian(3)
            second_step(2)
            done(second_step(3))
            for h in range(2):
                o = take_bank(pe, "WB", h).bitcast(bf16)
                for f in range(8):
                    last = t.transpose(o[:, 128 * f:128 * f + 128], winq_t[:, f, 128 * h:128 * h + 128], identb[:])
                done(last)

            vproj(0)
            pe.wait_ge(S["ab_ready"], 1)
            o = take_bank(pe, "IN", 0)
            done(t.matmul(o[0:NS, :], tb("J"), pr2.rearrange("p g c -> p (g c)"), start=True, stop=True))
            vproj(1)
            vproj(2)
            pe.wait_ge(S["own_ready"], 1)
            o = take_bank(pe, "ME", 0)
            for r in range(2):
                last = t.matmul(o[:, 0:NB], tb("FR", NS)[:, 128 * r:128 * r + 128], ins[:, r:NM:2],
                                start=(r == 0), stop=(r == 1))
            done(last)
            pe.wait_ge(S["mean_ready"], 1)
            o = take_bank(pe, "TM", 0)
            done(t.transpose(o[0:NB, 0:128], mean, tb("I")))
            vproj(3)
            pe.wait_ge(S["cand_ready"], 1)
            o = take_bank(pe, "BC", 0)
            done(t.matmul(o[:, 0:256], ones[0:NB, :], cand, start=True, stop=True))
            vproj(4)
            pe.wait_ge(S["eq_ready"], 1)
            o = take_bank(pe, "EQ", 0)
            done(t.matmul(o[:, 0:1], tb("L"), eqrow, start=True, stop=True))
            vproj(5)
            pe.wait_ge(S["wn_ready"], 1)
            o = take_bank(pe, "W1", 0)
            for r in range(2):
                last = t.matmul(o[0:NS, 16 * r:16 * r + 16], tb("FS")[:, NS * r:NS * r + NS], wn, start=True, stop=True)
            done(last)
            vproj(6)
            pe.wait_ge(S["w1_ready"], 1)
            o = take_bank(pe, "W2", 0)
            done(t.matmul(o, tb("JT", NS), own, start=True, stop=True))
            vproj(7)
            for i in range(8):
                pe.wait_ge(S["vh_ready"], i + 1)
                o = take_bank(pe, "VF", i)
                for m in range(2):
                    g = 2 * i + m
                    last = t.matmul(o[:, 256 * m:256 * m + 256], BU[:, g, :], xh[:, 256 * g:256 * g + 256],
                                    start=True, stop=True)
                done(last)

            def open_sums(lo, hi):
                pe.wait_ge(S["xb_ready"], 1)
                for i in range(lo, hi):
                    t.matmul(take_bank(pe, "IV", i), tb("I"), xs[:, 512 * i:512 * i + 512], start=True, stop=False)

            open_sums(0, 4)
            pe.wait_ge(S["nz_ready"], 1)
            for i in range(8):
                pe.wait_ge(S["vv_ready"], i + 1)
                pe.wait_ge(S["nm_ready"], i // 4 + 1)
                pe.wait_ge(S["nm_a"], i // 4 + 1)
                o = take_bank(pe, "OO", i)
                for m in range(2):
                    g = 2 * i + m
                    last = t.matmul(o[:, 256 * m:256 * m + 256], NM_[:, g, :], xt[:, 256 * g:256 * g + 256],
                                    start=True, stop=True)
                done(last)
            open_sums(4, 8)
            for i in range(8):
                pe.wait_ge(spec_in[i], 32 if i % 2 else 16)
            for i in range(4):
                pe.wait_ge(spec_sw[i], 16)
            for i in range(8):
                done(t.matmul(bank("IV", i), tb("FT"), ct[:, 512 * i:512 * i + 512], start=False, stop=True))
            for i in range(8):
                pe.wait_ge(S["y_a"], i // 2 + 1)
                pe.wait_ge(S["y_d"], i // 2 + 1)
                o = take_bank(pe, "TY", i)
                for h in range(2):
                    for m in range(2):
                        b = 2 * i + m
                        last = t.transpose(o[:, 256 * h + 128 * m:256 * h + 128 * m + 128],
                                           yn[:, 256 * b + 128 * h:256 * b + 128 * h + 128], tb("I"))
                done(last)
            pe.wait_ge(S["am_ready"], 1)
            o = take_bank(pe, "AM1", 0)
            done(t.transpose(o[0:1, 0:128], am, tb("I")))
            pe.wait_ge(S["a1_ready"], 1)
            o = take_bank(pe, "AM2", 0)
            done(t.matmul(o[:, 0:1], inv[:], a2, start=True, stop=True))
            pe.wait_ge(S["winq_ready"], 2)
            for n in range(0, 32, 4):
                c, f = n // 8, n % 8
                if n == 8:
                    pe.wait_ge(S["wom_ready"], 1)
                    o = take_bank(pe, "WG1", 0)
                    done(t.transpose(o[0:1, 0:128], wg, tb("I")))
                if n == 16:
                    pe.wait_ge(S["wg_ready"], 1)
                    o = take_bank(pe, "WG2", 0)
                    done(t.matmul(o[:, 0:1], ones[0:1, :], a1, start=True, stop=True))
                o = [take_bank(pe, "M1", n + k) for k in range(4)]
                pe.wait_ge(S["yhi_ready"], c + 1)
                for k in range(4):
                    for h in range(2):
                        fs = slice(128 * (f + k), 128 * (f + k) + 128)
                        t.matmul(o[k], winq[:, h, fs], yhi[:, h, 512 * c:512 * c + 512], start=(h == 0), stop=False)
                pe.wait_ge(S["yq_ready"], c + 1)
                for k in range(4):
                    for h in range(2):
                        fs = slice(128 * (f + k), 128 * (f + k) + 128)
                        last = t.matmul(o[k], winq[:, h, fs], ylo[:, h, 512 * c:512 * c + 512], start=False, stop=(h == 1))
                    done(last)
            pe.wait_ge(S["hm_ready"], 1)
            o = take_bank(pe, "HM1", 0)
            done(t.transpose(o[0:1, 0:128], am, tb("I")))
            pe.wait_ge(S["ha_ready"], 1)
            o = take_bank(pe, "HM2", 0)
            done(t.matmul(o[:, 0:1], inv[:], a3, start=True, stop=True))
            for c in range(4):
                o = [take_bank(pe, "M2", 4 * c + k) for k in range(4)]
                for f in range(8):
                    low = (Hlo5 if f < 4 else Hlo8)[:, f % 4]
                    pe.wait_ge(S["hhi_ready"], 4 * c + f // 2 + 1)
                    for k in range(4):
                        t0 = 128 * (4 * c + k)
                        t.matmul(o[k][:, 0:256], Hhi[:, f, t0:t0 + 128], woutq[:, f, :], start=(f == 0), stop=False)
                    pe.wait_ge(S["hq_ready"], 4 * c + f // 2 + 1)
                    for k in range(4):
                        t0 = 128 * (4 * c + k)
                        last = t.matmul(o[k][:, 0:256], low[:, t0:t0 + 128], woutq[:, f, :], start=False, stop=(f == 7))
                        if f == 7:
                            done(last)


def kernel(x, ctx_1024, L0_xattn_Wq, L0_xattn_bq, L0_xattn_Wk, L0_xattn_bk, L0_xattn_Wv, L0_xattn_bv,
           L0_xattn_Wo, L0_xattn_bo, L0_ffn_W_in, L0_ffn_b_in, L0_ffn_W_out, L0_ffn_b_out):
    import concourse.bacc as bacc
    from concourse.bass_utils import run_bass_kernel_spmd

    def cols(v):
        return np.asarray(v).reshape(-1, 128).T

    tab, at = shape_tables()
    arrays = {
        "x": x, "ctx_in": ctx_1024, "wqT": np.asarray(L0_xattn_Wq).T, "wkT": np.asarray(L0_xattn_Wk).T,
        "wvT": np.asarray(L0_xattn_Wv).T,
        "wo": L0_xattn_Wo, "winT": np.asarray(L0_ffn_W_in).T, "wout": L0_ffn_W_out,
        "cols": np.concatenate([cols(L0_xattn_bk), cols(L0_xattn_bq), cols(L0_xattn_bv), cols(L0_ffn_b_in)], 1),
        "rows": np.concatenate([np.asarray(L0_xattn_bo), np.asarray(L0_ffn_b_out)])[None],
        "tab": tab,
    }
    arrays = {k: np.ascontiguousarray(v) for k, v in arrays.items()}
    nc = bacc.Bacc("TRN2", target_bir_lowering=False, num_devices=1)
    aps = {k: nc.dram_tensor(k + "_dram", v.shape, mybir.dt.from_np(v.dtype), kind="ExternalInput").ap()
           for k, v in arrays.items()}
    out = nc.dram_tensor("out_dram", (1, T, D), mybir.dt.float32, kind="ExternalOutput").ap()
    build(nc, out=out, at=at, **aps)
    r = run_bass_kernel_spmd(nc, [{k + "_dram": v for k, v in arrays.items()}], core_ids=[0])
    return r.results[0]["out_dram"]
```

```python
import concourse.bass as bass
from concourse import mybir
from contextlib import ExitStack
import numpy as np

T = 2048
TC = 1601
D = 256
FF = 1024
NA, NB = 128, 16
NS, NG, NJ = 64, 16, 4
NM = 32
TOPK = int(2 * np.log(T))
AF = TC // NB


def shape_tables():
    a, b = np.arange(NA), np.arange(NB)
    F = np.zeros((NA, NS, 2))
    for s in range(NS):
        F[:, s, 0] = np.cos(2 * np.pi * ((s * a) % NA) / NA)
        F[:, s, 1] = -np.sin(2 * np.pi * ((s * a) % NA) / NA)
    F[:, 0, 1] = 1.0 - 2.0 * (a % 2)
    U = np.zeros((NS, NM, NB, 2))
    V = np.zeros((NS, NM, NB, 2))
    sign = np.ones((NS, NM))
    for s in range(NS):
        for m in range(NM):
            k, part = m // 2, m % 2
            if s:
                f, w = s + NA * k, 2
            elif k == 0:
                f, w, part, src = (T // 2) * part, 1, 0, 0
            elif k < 8:
                f, w, src = NA * k, 2, 0
            else:
                f, w, src = NA // 2 + NA * (k - 8), 2, 1
            th = 2 * np.pi * ((f * b) % T) / T
            c, n = np.cos(th), -np.sin(th)
            if s:
                U[s, m, :, 0], U[s, m, :, 1] = (c, -n) if part == 0 else (n, c)
            else:
                U[s, m, :, src] = c if part == 0 else n
            V[s, m] = U[s, m] * w / T
            if part:
                sign[s, m] = 1.0 if f > T // 2 else -1.0
    P = V * (sign / D)[:, :, None, None]
    UR, UI, W = np.zeros_like(U), np.zeros_like(U), np.zeros_like(V)
    for m in range(NM):
        UR[:, m], UI[:, m] = U[:, m - m % 2], U[:, m - m % 2 + 1]
        W[:, m] = -V[:, m + 1] if m % 2 == 0 else V[:, m - 1]
    UR[0, 1], UI[0, 0:2], W[0, 0:2] = U[0, 1], 0, 0
    rows = [AF + 1 if x < TC - AF * NB else AF for x in range(NB)]
    ind = np.stack([F[0:rows[x]].sum(0) for x in range(NB)], 1)

    def by_row(x):
        return x.reshape(NG, NJ, NM, 32).transpose(1, 2, 0, 3).reshape(128, -1)

    out = {
        "F": F.reshape(NA, 128),
        "UT": U.reshape(NG, NJ, NM, 32).transpose(1, 3, 0, 2).reshape(128, -1),
        "IND": ind.reshape(NG, 128).T,
        "INDF": np.einsum("smbr,sbr->sm", U, ind).reshape(NG, 128).T,
        "U": by_row(U), "P": by_row(P),
        "FR": np.concatenate([F.reshape(NA, NG, NJ, 2).transpose(2, 1, 3, 0).reshape(NS, 256), np.zeros((64, 256))], 0),
        "J": np.kron(np.eye(NJ), np.ones((NM, NG))),
        "JT": np.concatenate([np.kron(np.eye(NJ), np.ones((NG, NM))), np.zeros((64, 128))], 0),
        "G": np.concatenate([np.tile(np.eye(NG), (NJ, 1)), np.zeros((64, NG))], 0),
        "UR": by_row(UR), "UI": by_row(UI), "V": by_row(V), "W": by_row(W),
        "FT": F.transpose(1, 2, 0).reshape(128, NA),
        "I": np.eye(128),
        "L": np.triu(np.ones((128, 128)), 1),
        "DK": np.concatenate([np.kron(np.eye(NB), np.ones((1, NB))), np.zeros((112, 256))], 0),
        "FS": F.reshape(NA, NG, NJ, 2).transpose(0, 3, 2, 1).reshape(NA, 128),
    }
    at, pos = {}, 0
    for k, x in out.items():
        at[k] = (pos, pos + x.shape[1])
        pos += x.shape[1]
    return np.concatenate(list(out.values()), 1).astype(np.float32), at


def build(nc, x, ctx_in, wqT, wkT, wvT, wo, winT, wout, cols, rows, tab, out, at):
    f32, bf16, f16 = mybir.dt.float32, mybir.dt.bfloat16, mybir.dt.float16
    ALU, ACT, AX = mybir.AluOpType, mybir.ActivationFunctionType, mybir.AxisListType
    MAGIC = 12582912.0
    TAKEN = -3.3e38
    NCONST = tab.shape[1]
    es = ExitStack()
    with es:
        SL = 4096
        arena = es.enter_context(nc.sbuf_tensor("arena", [128, 9 * SL], f32))

        def slot(n, cols=SL, skip=0):
            return arena[:, n * SL + skip:n * SL + skip + cols]

        xs = slot(0)
        cx = slot(1)
        xh = slot(2)
        xt = slot(3)
        BU = slot(4, 2048).rearrange("p (g c) -> p g c", g=NG)
        NM_ = slot(4, 2048, 2048).rearrange("p (g c) -> p g c", g=NG)
        BUT = slot(3, 2048).rearrange("p (g c) -> p g c", g=NG)
        MIX = slot(3, 2048, 2048).rearrange("p (g c) -> p g c", g=NG)
        ct = slot(5)
        yn = slot(6)
        qt = slot(7)
        wraw = slot(8)
        H = arena[:, 1 * SL:5 * SL].rearrange("p (f t) -> p f t", f=8)
        Hhi = arena[:, 6 * SL:8 * SL].bitcast(f16).rearrange("p (f t) -> p f t", f=8)
        Hlo5 = slot(5).bitcast(f16).rearrange("p (f t) -> p f t", f=4)
        Hlo8 = slot(8).bitcast(f16).rearrange("p (f t) -> p f t", f=4)
        yhi = slot(5, 2048).bitcast(bf16).rearrange("p (h t) -> p h t", h=2)
        ylo = slot(5, 2048, 2048).bitcast(bf16).rearrange("p (h t) -> p h t", h=2)

        def sb(name, shape, dt=f32):
            return es.enter_context(nc.sbuf_tensor(name, shape, dt))

        tabs = sb("tabs", [128, NCONST])

        def tb(name, p=128):
            return tabs[0:p, at[name][0]:at[name][1]]

        def tb3(name):
            return tb(name).rearrange("p (g c) -> p g c", g=NG)

        wqT_s, wkT_s, wvT_s, wo_s = (slot(6, 512, 512 * i).rearrange("p (h n) -> p h n", h=2) for i in range(4))
        wqk, wvo = sb("wqk", [128, 2, D]), sb("wvo", [128, 2, D])
        wqbk = sb("wqbk", [128, D])
        bvo = sb("bvo", [128, D])
        bkb = slot(6, 256, 2048).rearrange("p (h n) -> p h n", h=2)
        bvb = slot(6, 256, 2304).rearrange("p (h n) -> p h n", h=2)
        winq = sb("winq", [128, 2, FF], bf16)
        woutq = sb("woutq", [128, 8, D], f16)
        colv = sb("colv", [128, 14])
        rowv = sb("rowv", [128, 2 * D])
        scr = sb("scr", [128, 4, 1024])
        scr16 = scr[:].rearrange("p n c -> p (n c)").bitcast(mybir.dt.int16)\
                      .rearrange("p (n c two) -> p n c two", n=4, two=2)[:, :, :, 0]
        winq_t = wraw[:, 0:1024].bitcast(bf16).rearrange("p (f d) -> p f d", f=8)
        wtmp = scr[:, 3, 0:D]
        gram = scr[:, 0, 0:512].rearrange("p (g c) -> p g c", g=NG)
        pr1 = scr[:, 0, 512:1024].rearrange("p (g c) -> p g c", g=NG)
        pr2 = scr[:, 1, 0:512].rearrange("p (g c) -> p g c", g=NG)
        own = scr[0:NS, 1, 512:1024]
        ownq = scr[0:NS, 3, 256:768]
        ins = sb("ins", [NS, NM])
        sm = sb("sm", [128, 704])
        sq = [0]

        def small(n, p=128):
            sq[0] += n
            return sm[0:p, sq[0] - n:sq[0]]

        eps, one, posM, mhalf, ve = *(small(1) for _ in range(4)), small(4)
        bqk, bqbk, qb, qbs = small(2), small(1), small(16), small(16)
        st = small(96).rearrange("p (b k) -> p b k", b=NB)
        mv = small(32).rearrange("p (b k) -> p b k", b=NB)
        sd, rs, nt, nmr = small(16), small(16), small(16), small(16)
        warm = small(2)
        ab, mean, ex, wn, eq, pre, gone = (small(16) for _ in range(7))
        negmx, zr, rz, eqrow, neq = (small(1) for _ in range(5))
        m16 = small(16, NB)
        v16, exv, eqv = small(16), small(16), small(16)
        cand = scr[0:NB, 2, 0:256]
        left = scr[0:NB, 2, 256:256 + 128]
        left2 = scr[:, 2, 512:512 + 256]
        r1, r2 = small(16), small(16)
        wx, wm, wom = small(8), small(8), small(8)
        rf, hrf, wg, rwg = small(8), small(8), small(1), small(1)
        ss1, ss2 = small(8), small(8)
        ym, hm, am, yb, hb = small(4), small(17), small(1), small(1), small(1)
        ysc, hsc, sc1, sc2 = small(1), small(1), small(8), small(1)
        a1, a2, a3 = small(1, 1), small(1, 1), small(1, 1)
        ones = sb("ones", [128, 128])
        inv = sb("inv", [1, 128])
        identb = sb("identb", [128, 128], bf16)

        ps = es.enter_context(nc.psum_tensor("ps", [128, 8, 512], f32))

        def sem(name):
            return es.enter_context(nc.semaphore(name))

        names = ("ld_F ld_wqk ld_tab ld_wv ld_win ld_wout ld_col ld_row "
                 "pe dve_link act_link pool_const bu_ready bo_ready bt_zero x2b_ready nz_ready "
                 "xh_a xh_d qt_ready wqk_ready qc_ready bkb_ready qb_ready ownq_ready qbs_ready wvo_ready bvo_ready bvb_ready gram_a gram_d ab_ready own_ready "
                 "mean_ready cand_ready v16_ready ex_ready eq_ready wn_ready "
                 "w1_ready vh_ready mix_ready bt_ready w2_ready nm_ready os_a os_d x2_d x2_ready sd_ready "
                 "var_ready rs_ready y_a y_d yt_ready am_ready a1_ready ysc_ready winq_ready "
                 "wom_ready wg_ready rf_ready yu_ready yhi_ready yq_ready h_ready hm_ready ha_ready hsc_ready "
                 "yq_scale hhi_first hu_a hu_d hu_p nm_a nm_c hhi_ready hq_ready o_ready out_done ct_ready ones_ready rs2_ready pool_chain xt_a xt_d identb_ready").split()
        S = {n: sem(n) for n in names}
        ld_ctx = [sem(f"ld_ctx{i}") for i in range(5)]
        ld_rest = sem("ld_rest")
        ld_xs = [sem(f"ld_x{i}") for i in range(4)]
        spec_in = [sem(f"spec_in{i}") for i in range(8)]
        spec_sw = [sem(f"spec_sw{i}") for i in range(4)]

        OPENED = 2

        def x2_by(i):
            return (S["x2_d"], i + 1) if i < OPENED else (S["x2_ready"], i - OPENED + 1)

        order = []
        order += [("HT", 0)] + [("CD", i) for i in range(8)] + [("GG", 0), ("SM", 0)]
        order += [("XD", i) for i in range(4)] + [("WVO", 0)] + [("XD", i) for i in range(4, 8)] + [("BVO", 0)] + [("QP", i) for i in range(8)]
        order += [("QB1", 0), ("GR", 0), ("GR", 1), ("QB2", 0), ("GR", 2), ("GR", 3), ("UU", 0), ("WB", 0), ("WB", 1)]
        order += [("VP", 0), ("IN", 0), ("VP", 1), ("ME", 0), ("TM", 0), ("VP", 2), ("BC", 0)]
        order += [("VP", 3), ("EQ", 0), ("VP", 4), ("W1", 0), ("W2", 0), ("VP", 5), ("VP", 6)]
        order += [("MX", 0), ("MX", 1), ("VP", 7), ("OO", 0), ("OO", 1), ("MX", 2), ("MX", 3)]
        order += [("OO", i) for i in range(2, 8)] + [("IV", i) for i in range(8)]
        for i in range(0, 8, 2):
            order += [("TY", i), ("TY", i + 1), ("HT", 1 + i // 2)]
        order += [("AM1", 0), ("AM2", 0), ("HT", 5)]
        order += [("M1", i) for i in range(8)] + [("WG1", 0)] + [("M1", i) for i in range(8, 16)] + [("WG2", 0)]
        order += [("M1", i) for i in range(16, 32)] + [("HT", 6), ("HM1", 0), ("HM2", 0), ("HT", 7)]
        order += [("M2", i) for i in range(8)]
        nth = {u: n for n, u in enumerate(order)}

        emptied = {
            "HT": lambda i: [],
            "CD": lambda i: [(S["ct_ready"], i + 1)],
            "GG": lambda i: [(S["wqk_ready"], 1)],
            "SM": lambda i: [(S["qc_ready"], 1)],
            "QB1": lambda i: [(S["ownq_ready"], 1)],
            "QB2": lambda i: [(S["qbs_ready"], 1)],
            "XD": lambda i: [(S["xt_a" if i % 2 == 0 else "xt_d"], i // 2 + 1)],
            "QP": lambda i: [(S["qt_ready"], i + 1)],
            "GR": lambda i: [(S["gram_a"], i + 1), (S["gram_d"], i + 1)],
            "WVO": lambda i: [(S["wvo_ready"], 1)],
            "BVO": lambda i: [(S["bvo_ready"], 1)],
            "UU": lambda i: [(S["ab_ready"], 1)],
            "VP": lambda i: [(S["vh_ready"], i + 1)],
            "IN": lambda i: [(S["own_ready"], 1)],
            "ME": lambda i: [(S["mean_ready"], 1)],
            "MX": lambda i: [(S["mix_ready"], i + 1)],
            "WG1": lambda i: [(S["wg_ready"], 1)],
            "WG2": lambda i: [(S["rf_ready"], 1)],
            "WB": lambda i: [(S["winq_ready"], i + 1)],
            "TM": lambda i: [(S["cand_ready"], 1)],
            "BC": lambda i: [(S["v16_ready"], 1)],
            "EQ": lambda i: [(S["wn_ready"], 1)],
            "W1": lambda i: [(S["w1_ready"], 1)],
            "W2": lambda i: [(S["w2_ready"], 2)],
            "OO": lambda i: [(S["os_a" if i % 2 == 0 else "os_d"], i // 2 + 1)],
            "IV": lambda i: [x2_by(i)],
            "TY": lambda i: [(S["yt_ready"], i + 1)],
            "AM1": lambda i: [(S["a1_ready"], 1)],
            "AM2": lambda i: [(S["ysc_ready"], 1)],
            "M1": lambda i: [(S["h_ready"], i + 1)],
            "HM1": lambda i: [(S["ha_ready"], 1)],
            "HM2": lambda i: [(S["hsc_ready"], 1)],
            "M2": lambda i: [(S["o_ready"], i + 1)],
        }

        ACT_SHARE = (2, 3, 3, 2)
        DVE_ROUNDS = (0, 1, 3, 7, 11)
        POOL_ROUNDS = (5, 9, 13)

        def piece(h, n):
            return h[:, n % 8, 1024 * (n // 8):1024 * (n // 8) + 1024]

        def rounded_by(n):
            by_dve, by_pool = sum(k <= n for k in DVE_ROUNDS), sum(k <= n for k in POOL_ROUNDS)
            if n in DVE_ROUNDS:
                return S["hu_d"], by_dve
            return (S["hu_p"], by_pool) if n in POOL_ROUNDS else (S["hu_a"], n + 1 - by_dve - by_pool)

        def bank(stage, i):
            return ps[:, nth[stage, i] % 8, :]

        def filled(eng, stage, i):
            eng.wait_ge(S["pe"], nth[stage, i] + 1)

        def take_bank(pe, stage, i):
            n = nth[stage, i]
            if n >= 8:
                prev, k = order[n - 8]
                for s, v in emptied[prev](k):
                    pe.wait_ge(s, v)
            return bank(stage, i)

        block = es.enter_context(nc.Block())

        @block.sync
        def _(sp):
            c3 = ctx_in[0, 0:AF * NB, :].rearrange("(a b) d -> a b d", b=NB)
            cs = cx.rearrange("p (b d) -> p b d", b=NB)
            sp.dma_start(tb("F"), tab[:, at["F"][0]:at["F"][1]]).then_inc(S["ld_F"], 16)
            sp.dma_start(cs[0:AF, 0:2, :], c3[:, 0:2, :]).then_inc(ld_ctx[0], 16)
            sp.dma_start(cs[AF:AF + 1, 0, :], ctx_in[0, AF * NB:TC, :]).then_inc(ld_ctx[4], 16)
            sp.dma_start(cs[0:AF, 2:4, :], c3[:, 2:4, :]).then_inc(ld_rest, 16)
            for i in range(1, 4):
                sp.dma_start(cs[0:AF, 4 * i:4 * i + 4, :], c3[:, 4 * i:4 * i + 4, :]).then_inc(ld_ctx[i], 16)
            sp.dma_start(colv[:], cols).then_inc(S["ld_col"], 16)
            x3 = x[0].rearrange("(a b) d -> a (b d)", b=NB)
            for i in range(4):
                sp.dma_start(xs[:, 1024 * i:1024 * i + 1024], x3[:, 1024 * i:1024 * i + 1024]).then_inc(ld_xs[i], 16)
                if i == 1:
                    for w_s, w in ((wqT_s, wqT), (wkT_s, wkT)):
                        sp.dma_start(w_s, w.rearrange("(h p) n -> p h n", p=128)).then_inc(S["ld_wqk"], 16)
            sp.dma_start(wvT_s, wvT.rearrange("(h p) n -> p h n", p=128)).then_inc(S["ld_wv"], 16)
            sp.dma_start(wo_s, wo.rearrange("(h p) n -> p h n", p=128)).then_inc(S["ld_wv"], 16)
            sp.dma_start(tabs[:, at["UT"][0]:NCONST], tab[:, at["UT"][0]:NCONST]).then_inc(S["ld_tab"], 16)
            sp.dma_start(rowv[:], rows[0:1, :].to_broadcast([128, 2 * D])).then_inc(S["ld_row"], 16)
            sp.dma_start(wraw[:, 0:2048].rearrange("p (f d) -> p f d", f=8),
                         winT.rearrange("(f p) d -> p f d", p=128)).then_inc(S["ld_win"], 16)
            sp.dma_start(wraw[:, 2048:4096].rearrange("p (f d) -> p f d", f=8),
                         wout.rearrange("(f p) d -> p f d", p=128)).then_inc(S["ld_wout"], 16)
            os3 = cx.rearrange("p (g c) -> p g c", g=NG)
            or3 = ct.rearrange("p (b c) -> p b c", b=NB)
            for i in range(8):
                sp.wait_ge(S["os_a" if i % 2 == 0 else "os_d"], i // 2 + 1)
                for g in (2 * i, 2 * i + 1) if i % 2 else (2 * i,) if i else ():
                    sp.dma_start(or3[8 * g:8 * g + 8], os3[:, g, :]).then_inc(spec_in[i], 16)
                if i == 1:
                    sp.wait_ge(S["bo_ready"], 1)
                    sp.dma_start(or3[0:8], os3[:, 0, :]).then_inc(spec_in[0], 16)
            o3 = out[0].rearrange("(a b) d -> a (b d)", b=NB)
            for i in range(8):
                sp.wait_ge(S["o_ready"], i + 1)
                sp.dma_start(o3[:, 512 * i:512 * i + 512], xs[:, 512 * i:512 * i + 512]).then_inc(S["out_done"], 16)
            sp.wait_ge(S["out_done"], 8 * 16)

        def reciprocal_root(e, lo, hi, chain, first):
            r, n_, w = rs[:, lo:hi], nt[:, lo:hi], mv[:, lo:hi, 1]
            chain(first)
            chain(e.scalar_tensor_tensor(out=n_, in0=w, scalar=1e-5, in1=r, op0=ALU.add, op1=ALU.mult))
            chain(e.scalar_tensor_tensor(out=n_, in0=n_, scalar=-0.5, in1=r, op0=ALU.mult, op1=ALU.mult))
            chain(e.scalar_tensor_tensor(out=r, in0=n_, scalar=1.5, in1=r, op0=ALU.add, op1=ALU.mult))
            return e.scalar_tensor_tensor(out=nmr[:, lo:hi], in0=mv[:, lo:hi, 0], scalar=-1.0, in1=r,
                                          op0=ALU.mult, op1=ALU.mult)

        @block.gpsimd
        def _(pool):
            g = nc.gpsimd
            chained = [0]

            def chain(ins_):
                chained[0] += 1
                ins_.then_inc(S["pool_chain"], 1)
                pool.wait_ge(S["pool_chain"], chained[0])

            g.memset(ones[:], 1.0).then_inc(S["ones_ready"], 1)
            pool.wait_ge(S["ones_ready"], 1)
            g.memset(one, 1.0)
            g.memset(inv[:], 1.0 / 32767.0)
            g.memset(posM, MAGIC)
            g.memset(eps, 1e-5)
            g.memset(mhalf, -0.5)
            g.memset(BU, 0.0).then_inc(S["pool_const"], 1)
            g.memset(NM_, 0.0).then_inc(S["nz_ready"], 1)
            pool.wait_ge(S["nz_ready"], 1)
            pool.wait_ge(S["ld_tab"], 16)
            g.tensor_copy(identb[:], tb("I")).then_inc(S["identb_ready"], 1)
            pool.wait_ge(S["identb_ready"], 1)
            filled(pool, "QP", 7)
            g.memset(BUT, 0.0).then_inc(S["bt_zero"], 1)
            pool.wait_ge(S["bt_zero"], 1)
            pool.wait_ge(S["ld_row"], 16)
            for i in range(0, 8, 2):
                pool.wait_ge(S["os_a"], i // 2 + 1)
                gg = 2 * i + 1
                g.dma_start(ct[8 * gg:8 * gg + 8, :].rearrange("p (b c) -> p b c", b=NB),
                            cx.rearrange("p (g c) -> p g c", g=NG)[:, gg, :]).then_inc(spec_sw[i // 2], 16)
                if i == 0:
                    g.tensor_tensor(cx[0:NB, 0:D], cx[0:NB, 0:D], rowv[0:NB, 0:D], ALU.add).then_inc(S["bo_ready"], 1)
                    pool.wait_ge(S["bo_ready"], 1)
            pool.wait_ge(S["var_ready"], 5)
            q = slice(8, 12)
            chain(g.tensor_scalar(ve, mv[:, q, 1], 1e-5, None, ALU.add))
            chain(g.tensor_tensor(rs[:, q], ve, mhalf.to_broadcast([128, 4]), ALU.pow))
            chain(g.tensor_tensor(nt[:, q], rs[:, q], rs[:, q], ALU.mult))
            chain(g.tensor_tensor(nt[:, q], nt[:, q], ve, ALU.mult))
            chain(g.tensor_scalar(nt[:, q], nt[:, q], -0.5, 1.5, ALU.mult, ALU.add))
            chain(g.tensor_tensor(rs[:, q], rs[:, q], nt[:, q], ALU.mult))
            chain(g.tensor_tensor(nmr[:, q], mv[:, q, 0], rs[:, q], ALU.mult))
            g.tensor_scalar(nmr[:, q], nmr[:, q], -1.0, None, ALU.mult).then_inc(S["rs2_ready"], 1)
            pool.wait_ge(S["rs2_ready"], 1)
            x3 = xs.rearrange("p (b d) -> p b d", b=NB)
            pool.wait_ge(S["yq_ready"], 4)
            g.tensor_tensor(x3, x3, rowv[:, D:2 * D].unsqueeze(1).to_broadcast([128, NB, D]), ALU.add).then_inc(S["x2b_ready"], 1)
            pool.wait_ge(S["hsc_ready"], 1)
            for n in POOL_ROUNDS:
                pool.wait_ge(S["hq_ready"], n - 3)
                g.tensor_scalar(scr[:, n % 4, :], piece(H, n), hsc, MAGIC, ALU.mult, ALU.add).then_inc(S["hu_p"], 1)

        def spread(buf, h, bq):
            v = buf[:, h * 2048:(h + 1) * 2048].rearrange("p (s b r) -> p b s r", b=NB, r=2)
            return v[:, 4 * bq:4 * bq + 4]

        @block.scalar
        def _(act):
            a = nc.scalar
            linked = [0]

            def link(ins_):
                linked[0] += 1
                ins_.then_inc(S["act_link"], 1)
                act.wait_ge(S["act_link"], linked[0])

            act.wait_ge(S["pool_const"], 1)
            a.activation(warm[:, 0:1], one, ACT.Sqrt)
            for i in range(8):
                filled(act, "CD", i)
                a.copy(spread(ct, i % 2, i // 2), bank("CD", i).rearrange("p (b s r) -> p b s r", b=4, r=2)).then_inc(S["ct_ready"], 1)
            x3 = xs.rearrange("p (b d) -> p b d", b=NB)
            xh3 = xh.rearrange("p (b d) -> p b d", b=NB)
            y3 = yn.rearrange("p (b d) -> p b d", b=NB)

            def normalise_x(k):
                act.wait_ge(S["var_ready"], k + 1)
                a.activation(sd[:, 8 * k:8 * k + 8], mv[:, 8 * k:8 * k + 8, 1], ACT.Sqrt, bias=eps).then_inc(S["sd_ready"], 1)
                act.wait_ge(S["rs_ready"], k + 1)
                for b in range(8 * k + 4, 8 * k + 8):
                    ins_ = a.activation(xh3[:, b, :], x3[:, b, :], ACT.Identity, bias=nmr[:, b:b + 1], scale=rs[:, b:b + 1])
                ins_.then_inc(S["xh_a"], 1)

            normalise_x(0)
            filled(act, "GG", 0)
            a.copy(wqk[:].rearrange("p h n -> p (h n)"), bank("GG", 0)).then_inc(S["wqk_ready"], 1)
            filled(act, "SM", 0)
            link(a.copy(wqbk[:], bank("SM", 0)[:, 0:D]))
            link(a.copy(bqbk, bank("SM", 0)[:, D + 2:D + 3]))
            a.mul(bqk, bank("SM", 0)[:, D:D + 2], float(NA)).then_inc(S["qc_ready"], 1)
            normalise_x(1)
            for i in range(0, 8, 2):
                if i == 4:
                    filled(act, "WVO", 0)
                    a.copy(wvo[:].rearrange("p h n -> p (h n)"), bank("WVO", 0)).then_inc(S["wvo_ready"], 1)
                filled(act, "XD", i)
                a.copy(spread(xt, 0, i // 2), bank("XD", i).rearrange("p (b s r) -> p b s r", b=4, r=2)).then_inc(S["xt_a"], 1)
            filled(act, "BVO", 0)
            a.copy(bvo[:], bank("BVO", 0)[:, 0:D]).then_inc(S["bvo_ready"], 1)
            act.wait_ge(S["ld_tab"], 16)
            for j in range(NJ):
                q = slice(32 * j, 32 * j + 32)
                a.copy(BU[q, :, q], tb3("UT")[q]).then_inc(S["bu_ready"], 1)
            act.wait_ge(S["qc_ready"], 1)
            for i in range(8):
                h, c = i // 4, i % 4
                filled(act, "QP", i)
                dst = qt[:, h * 2048 + c * 512:h * 2048 + c * 512 + 512]
                src = bank("QP", i)
                if c == 0:
                    a.activation(dst[:, 0:32:2], src[:, 0:32:2], ACT.Identity, bias=bqk[:, h:h + 1])
                    a.copy(dst[:, 1:32:2], src[:, 1:32:2])
                    a.copy(dst[:, 32:512], src[:, 32:512]).then_inc(S["qt_ready"], 1)
                else:
                    a.copy(dst, src).then_inc(S["qt_ready"], 1)
            for i in range(4):
                filled(act, "GR", i)
                for j in (0, 1):
                    q = slice(32 * j, 32 * j + 32)
                    ins_ = a.copy(gram[q, 4 * i:4 * i + 4, :],
                                  bank("GR", i).rearrange("p (g c) -> p g c", g=4)[q, :, q])
                ins_.then_inc(S["gram_a"], 1)
            for i in range(2):
                filled(act, "WB", i)
                a.copy(winq[:, i, :], bank("WB", i).bitcast(bf16)).then_inc(S["winq_ready"], 1)
            act.wait_ge(S["bt_zero"], 1)
            for j in range(NJ):
                q = slice(32 * j, 32 * j + 32)
                a.copy(BUT[q, :, q], tb3("U")[q]).then_inc(S["bt_ready"], 1)
            a.activation(warm[:, 0:1], one, ACT.Exp)
            act.wait_ge(S["v16_ready"], 1)
            link(a.mul(negmx, v16[:, 0:1], -1.0))
            a.activation(exv[:, 0:TOPK], v16[:, 0:TOPK], ACT.Exp, bias=negmx, accum_out=zr)
            a.activation(ex, mean, ACT.Exp, bias=negmx).then_inc(S["ex_ready"], 1)

            def mixed(*units):
                for i in units:
                    filled(act, "MX", i)
                    a.copy(MIX[:, 4 * i:4 * i + 4, :].rearrange("p g c -> p (g c)"), bank("MX", i)).then_inc(S["mix_ready"], 1)

            def place(h):
                act.wait_ge(S["nm_c"], h + 1)
                gs = slice(8 * h, 8 * h + 8)
                for j in (0, 1):
                    q = slice(32 * j, 32 * j + 32)
                    ins_ = a.copy(NM_[q, gs, q].rearrange("p g (r b) -> p g b r", r=2),
                                  pr1[q, gs].rearrange("p g (b r) -> p g b r", r=2))
                ins_.then_inc(S["nm_a"], 1)

            place(0)
            mixed(0, 1)
            place(1)
            for i in range(0, 8, 2):
                if i == 2:
                    mixed(2, 3)
                filled(act, "OO", i)
                a.copy(cx[:, 512 * i:512 * i + 512], bank("OO", i)).then_inc(S["os_a"], 1)
            a.activation(warm[:, 0:1], one, ACT.Sqrt)

            def transposed(k):
                for i in (2 * k, 2 * k + 1):
                    filled(act, "TY", i)
                    a.copy(qt.rearrange("p (h t) -> p h t", h=2)[:, :, 256 * i:256 * i + 256],
                           bank("TY", i).rearrange("p (h t) -> p h t", h=2)).then_inc(S["yt_ready"], 1)

            def normalise(k):
                act.wait_ge(*(S["rs2_ready"], 1) if k == 2 else (S["rs_ready"], 4 if k == 3 else 3))
                for b in range(4 * k, 4 * k + ACT_SHARE[k]):
                    ins_ = a.activation(y3[:, b, :], x3[:, b, :], ACT.Identity, bias=nmr[:, b:b + 1], scale=rs[:, b:b + 1])
                ins_.then_inc(S["y_a"], 1)

            def x2_copy(*units):
                for i in units:
                    filled(act, "IV", i)
                    a.copy(xs[:, 512 * i:512 * i + 512], bank("IV", i)).then_inc(S["x2_ready"], 1)

            def deviation(lo, hi):
                act.wait_ge(S["var_ready"], hi + 2)
                a.activation(sd[:, 4 * lo:4 * hi], mv[:, 4 * lo:4 * hi, 1], ACT.Sqrt, bias=eps).then_inc(S["sd_ready"], 1)

            x2_copy(2, 3, 4)
            deviation(0, 2)
            x2_copy(5)
            normalise(0)
            x2_copy(6)
            normalise(1)
            x2_copy(7)
            transposed(0)
            deviation(3, 4)
            normalise(2)
            transposed(1)
            normalise(3)
            transposed(2)
            transposed(3)
            a.activation(warm[:, 1:2], one, ACT.Gelu)
            act.wait_ge(S["yq_scale"], 1)
            act.wait_ge(S["yt_ready"], 8)
            yt3 = qt.rearrange("p (h t) -> p h t", h=2)
            for h in range(2):
                a.mul(yhi[:, h, 0:512], yt3[:, h, 0:512], ysc).then_inc(S["yhi_ready"], 1)
            for c in range(1, 4):
                a.mul(yhi[:, :, 512 * c:512 * c + 512], yt3[:, :, 512 * c:512 * c + 512], ysc)\
                 .then_inc(S["yhi_ready"], 1)
            act.wait_ge(S["ysc_ready"], 1)
            for n in range(32):
                c, f = n // 8, n % 8
                filled(act, "M1", n)
                a.activation(H[:, f, 512 * c:512 * c + 512], bank("M1", n), ACT.Gelu,
                             bias=colv[:, 6 + f:7 + f], scale=sc1[:, f:f + 1]).then_inc(S["h_ready"], 1)
            act.wait_ge(S["hsc_ready"], 1)

            def rounded(n):
                if n >= 4:
                    act.wait_ge(S["hq_ready"], n - 3)
                a.activation(scr[:, n % 4, :], piece(H, n),
                             ACT.Identity, bias=posM, scale=hsc).then_inc(S["hu_a"], 1)

            def high(n):
                if n == 0:
                    a.mul(piece(Hhi, 0)[:, 0:512], piece(H, 0)[:, 0:512], hrf[:, 0:1]).then_inc(S["hhi_first"], 1)
                    a.mul(piece(Hhi, 0)[:, 512:1024], piece(H, 0)[:, 512:1024], hrf[:, 0:1]).then_inc(S["hhi_ready"], 1)
                    return
                a.mul(piece(Hhi, n), piece(H, n), hrf[:, n % 8:n % 8 + 1]).then_inc(S["hhi_ready"], 1)

            for n in range(16):
                high(n)
                if n < 15 and n + 1 not in DVE_ROUNDS + POOL_ROUNDS:
                    rounded(n + 1)

        @block.vector
        def _(dve):
            v = nc.vector
            linked = [0]

            def link(ins_):
                linked[0] += 1
                ins_.then_inc(S["dve_link"], 1)
                dve.wait_ge(S["dve_link"], linked[0])

            x3 = xs.rearrange("p (b d) -> p b d", b=NB)
            xh3 = xh.rearrange("p (b d) -> p b d", b=NB)

            def vproj(i):
                filled(dve, "VP", i)
                for k in range(2):
                    gg = 2 * i + k
                    ins_ = v.scalar_tensor_tensor(out=xh[:, 256 * gg:256 * gg + 256], in0=bvo[:],
                                                  scalar=tb("IND")[:, gg:gg + 1],
                                                  in1=bank("VP", i)[:, 256 * k:256 * k + 256],
                                                  op0=ALU.mult, op1=ALU.add)
                ins_.then_inc(S["vh_ready"], 1)

            def spread_bins(dst, src):
                return v.tensor_tensor(dst.rearrange("s (g b r) -> s g b r", g=NG, r=2),
                                       src[0:NS, 0:NM].rearrange("s (r b) -> s b r", r=2).unsqueeze(1).to_broadcast([NS, NG, NB, 2]),
                                       tb("G", NS).unsqueeze(2).unsqueeze(3).to_broadcast([NS, NG, NB, 2]), ALU.mult)

            def normalise_x(k):
                dve.wait_ge(S["sd_ready"], k + 1)
                reciprocal_root(v, 8 * k, 8 * k + 8, link, v.reciprocal(rs[:, 8 * k:8 * k + 8], sd[:, 8 * k:8 * k + 8])).then_inc(S["rs_ready"], 1)
                for b in range(8 * k, 8 * k + 4):
                    ins_ = v.tensor_scalar(xh3[:, b, :], x3[:, b, :], mv[:, b, 0:1], rs[:, b:b + 1], ALU.subtract, ALU.mult)
                ins_.then_inc(S["xh_d"], 1)

            dve.wait_ge(S["ld_col"], 16)
            v.tensor_copy(bkb, colv[:, 0:2].unsqueeze(2).to_broadcast([128, 2, 128])).then_inc(S["bkb_ready"], 1)
            v.tensor_copy(bvb, colv[:, 4:6].unsqueeze(2).to_broadcast([128, 2, 128])).then_inc(S["bvb_ready"], 1)

            def statistics_x(*chunks):
                for i in chunks:
                    dve.wait_ge(ld_xs[i], 16)
                    for b in range(4 * i, 4 * i + 4):
                        ins_ = v.bn_stats(st[:, b, :], x3[:, b, :])
                    if i % 2:
                        link(ins_)
                        for b in range(4 * i - 4, 4 * i + 4):
                            ins_ = v.bn_aggr(mv[:, b, :], st[:, b, :])
                        ins_.then_inc(S["var_ready"], 1)

            statistics_x(0, 1)
            dve.wait_ge(S["var_ready"], 1)
            normalise_x(0)
            statistics_x(2, 3)
            dve.wait_ge(S["var_ready"], 2)
            normalise_x(1)
            for k in range(1, 8, 2):
                filled(dve, "XD", k)
                v.tensor_copy(spread(xt, 1, k // 2), bank("XD", k).rearrange("p (b s r) -> p b s r", b=4, r=2))\
                 .then_inc(S["xt_d"], 1)
            dve.wait_ge(S["qc_ready"], 1)
            dve.wait_ge(S["xh_a"], 2)
            for b in range(NB):
                ins_ = v.tensor_tensor_reduce(out=cx[:, 256 * b:256 * b + 256], in0=xh3[:, b, :], in1=wqbk[:], scale=1.0, scalar=0.0,
                                              op0=ALU.mult, op1=ALU.add, accum_out=qb[:, b:b + 1])
            link(ins_)
            v.tensor_scalar(qb, qb, bqbk, None, ALU.add).then_inc(S["qb_ready"], 1)
            dve.wait_ge(S["ld_win"], 16)
            win3 = wraw[:, 0:2048].rearrange("p (f d) -> p f d", f=8)
            wou3 = wraw[:, 2048:4096].rearrange("p (f d) -> p f d", f=8)
            link(v.tensor_reduce(wx, win3, AX.X, ALU.max, apply_absolute_value=True))
            link(v.tensor_scalar(wx, wx, 1e-8, None, ALU.max))
            link(v.reciprocal(ss1, wx))
            link(v.tensor_scalar(ss1, ss1, 127.0, None, ALU.mult))
            for f in range(8):
                link(v.tensor_scalar(wtmp, win3[:, f, :], ss1[:, f:f + 1], MAGIC, ALU.mult, ALU.add))
                link(v.tensor_scalar(winq_t[:, f, :], wtmp, MAGIC, None, ALU.subtract))
            dve.wait_ge(S["ld_tab"], 16)
            filled(dve, "QB1", 0)
            spread_bins(ownq, bank("QB1", 0)).then_inc(S["ownq_ready"], 1)
            for i in range(4):
                if i == 2:
                    filled(dve, "QB2", 0)
                    link(v.tensor_tensor(pr1, bank("QB2", 0).rearrange("p (g c) -> p g c", g=NG), tb3("U"), ALU.mult))
                    link(v.tensor_reduce(qbs, pr1, AX.X, ALU.add))
                    v.tensor_tensor(qbs, qbs, tb("INDF"), ALU.mult).then_inc(S["qbs_ready"], 1)
                filled(dve, "GR", i)
                for j in (2, 3):
                    q = slice(32 * j, 32 * j + 32)
                    ins_ = v.tensor_copy(gram[q, 4 * i:4 * i + 4, :],
                                         bank("GR", i).rearrange("p (g c) -> p g c", g=4)[q, :, q])
                ins_.then_inc(S["gram_d"], 1)
            filled(dve, "UU", 0)
            link(v.tensor_tensor(pr1, bank("UU", 0).rearrange("p (g c) -> p g c", g=NG), tb3("U"), ALU.mult))
            link(v.tensor_reduce(ab, pr1, AX.X, ALU.add))
            dve.wait_ge(S["qbs_ready"], 1)
            link(v.tensor_tensor(ab, ab, qbs, ALU.add))
            v.tensor_tensor(pr2, tb3("P"), ab.unsqueeze(2).to_broadcast([128, NG, 32]), ALU.mult)\
             .then_inc(S["ab_ready"], 1)

            dve.wait_ge(S["bvo_ready"], 1)
            vproj(0)
            filled(dve, "IN", 0)
            link(v.tensor_tensor(own.rearrange("s (g c) -> s g c", g=NG), bank("IN", 0)[0:NS, :].rearrange("s (g c) -> s g c", g=NG),
                                 tb("G", NS).unsqueeze(2).to_broadcast([NS, NG, NM]), ALU.mult))
            v.tensor_reduce(ins[:], own.rearrange("s (g c) -> s c g", g=NG), AX.X, ALU.add).then_inc(S["own_ready"], 1)
            vproj(1)
            filled(dve, "ME", 0)
            v.tensor_copy(mean, bank("ME", 0)[:, 0:NB]).then_inc(S["mean_ready"], 1)
            filled(dve, "TM", 0)
            tm = bank("TM", 0)[0:NB, 0:128]
            link(v.max(m16[:, 0:8], tm))
            link(v.match_replace(left, m16[:, 0:8], tm, TAKEN))
            link(v.max(m16[:, 8:16], left))
            v.tensor_tensor(cand.rearrange("p (k i) -> p k i", k=NB), m16.unsqueeze(1).to_broadcast([NB, NB, NB]),
                            tb("DK", NB).rearrange("p (k i) -> p k i", k=NB), ALU.mult).then_inc(S["cand_ready"], 1)
            vproj(2)
            filled(dve, "BC", 0)
            bc = bank("BC", 0)[:, 0:256]
            link(v.max(v16[:, 0:8], bc))
            link(v.match_replace(left2, v16[:, 0:8], bc, TAKEN))
            v.max(v16[:, 8:16], left2).then_inc(S["v16_ready"], 1)
            dve.wait_ge(S["v16_ready"], 1)
            last_v = v16[:, TOPK - 1:TOPK]
            link(v.tensor_scalar(eq, mean, last_v, None, ALU.is_equal))
            v.reduce_sum(eqrow, eq, AX.X).then_inc(S["eq_ready"], 1)
            link(v.tensor_scalar(eqv[:, 0:TOPK], v16[:, 0:TOPK], last_v, None, ALU.is_equal))
            link(v.reduce_sum(neq, eqv[:, 0:TOPK], AX.X))
            dve.wait_ge(S["ex_ready"], 1)
            link(v.reciprocal(rz, zr))
            filled(dve, "EQ", 0)
            link(v.tensor_tensor_scan(pre, ones[:, 0:NB], eq, bank("EQ", 0)[:, 0:1], ALU.mult, ALU.add))
            link(v.scalar_tensor_tensor(out=gone, in0=pre, scalar=neq, in1=eq, op0=ALU.is_le, op1=ALU.mult))
            link(v.scalar_tensor_tensor(out=gone, in0=mean, scalar=last_v, in1=gone, op0=ALU.is_gt, op1=ALU.add))
            v.scalar_tensor_tensor(out=wn, in0=gone, scalar=rz, in1=ex, op0=ALU.mult, op1=ALU.mult)\
             .then_inc(S["wn_ready"], 1)
            filled(dve, "W1", 0)
            spread_bins(own, bank("W1", 0)).then_inc(S["w1_ready"], 1)
            vproj(3)
            filled(dve, "W2", 0)
            w2 = bank("W2", 0).rearrange("p (g c) -> p g c", g=NG)
            for h in range(2):
                gs = slice(8 * h, 8 * h + 8)
                v.tensor_tensor(pr1[:, gs], w2[:, gs], tb3("UR")[:, gs], ALU.mult)
                v.tensor_tensor(pr2[:, gs], w2[:, gs], tb3("UI")[:, gs], ALU.mult).then_inc(S["w2_ready"], 1)
                dve.wait_ge(S["w2_ready"], h + 1)
                v.tensor_reduce(r1[:, gs], pr1[:, gs], AX.X, ALU.add)
                link(v.tensor_reduce(r2[:, gs], pr2[:, gs], AX.X, ALU.add))
                v.tensor_tensor(pr1[:, gs], tb3("V")[:, gs], r1[:, gs].unsqueeze(2).to_broadcast([128, 8, 32]), ALU.mult)
                link(v.tensor_tensor(pr2[:, gs], tb3("W")[:, gs], r2[:, gs].unsqueeze(2).to_broadcast([128, 8, 32]), ALU.mult))
                v.tensor_tensor(pr1[:, gs], pr1[:, gs], pr2[:, gs], ALU.add).then_inc(S["nm_c"], 1)
                dve.wait_ge(S["nm_c"], h + 1)
                for j in (2, 3):
                    q = slice(32 * j, 32 * j + 32)
                    ins_ = v.tensor_copy(NM_[q, gs, q].rearrange("p g (r b) -> p g b r", r=2),
                                         pr1[q, gs].rearrange("p g (b r) -> p g b r", r=2))
                ins_.then_inc(S["nm_ready"], 1)
                if h == 0:
                    vproj(4)
                    vproj(5)
                else:
                    vproj(6)
                    vproj(7)

            def os_copy(i):
                filled(dve, "OO", i)
                v.tensor_copy(cx[:, 512 * i:512 * i + 512], bank("OO", i)).then_inc(S["os_d"], 1)

            os_copy(1)
            dve.wait_ge(S["ld_wout"], 16)
            link(v.tensor_reduce(wom, wou3, AX.X, ALU.max, apply_absolute_value=True))
            os_copy(3)
            link(v.tensor_scalar(wom, wom, 1e-8, None, ALU.max))
            v.tensor_reduce(wg, wom, AX.X, ALU.max).then_inc(S["wom_ready"], 1)
            link(v.reciprocal(ss2, wom))
            link(v.tensor_scalar(ss2, ss2, 127.0, None, ALU.mult))
            os_copy(5)
            os_copy(7)
            for f in range(8):
                link(v.tensor_scalar(wtmp, wou3[:, f, :], ss2[:, f:f + 1], MAGIC, ALU.mult, ALU.add))
                link(v.tensor_scalar(woutq[:, f, :], wtmp, MAGIC, None, ALU.subtract))
            for i in range(OPENED):
                filled(dve, "IV", i)
                v.tensor_tensor(xs[:, 512 * i:512 * i + 512], bank("IV", i), xs[:, 512 * i:512 * i + 512], ALU.add)\
                 .then_inc(S["x2_d"], 1)
            y3 = yn.rearrange("p (b d) -> p b d", b=NB)

            def statistics(k):
                for i in (2 * k, 2 * k + 1):
                    dve.wait_ge(*x2_by(i))
                    for b in (2 * i, 2 * i + 1):
                        ins_ = v.bn_stats(st[:, b, :], x3[:, b, :])
                link(ins_)
                for b in range(4 * k, 4 * k + 4):
                    ins_ = v.bn_aggr(mv[:, b, :], st[:, b, :])
                ins_.then_inc(S["var_ready"], 1)

            def roots(lo, hi, n):
                dve.wait_ge(S["sd_ready"], n)
                reciprocal_root(v, 4 * lo, 4 * hi, link, v.reciprocal(rs[:, 4 * lo:4 * hi], sd[:, 4 * lo:4 * hi]))\
                    .then_inc(S["rs_ready"], 1)
                dve.wait_ge(S["rs_ready"], n)

            def normalise(k):
                for b in range(4 * k + ACT_SHARE[k], 4 * k + 4):
                    ins_ = v.tensor_scalar(y3[:, b, :], x3[:, b, :], mv[:, b, 0:1], rs[:, b:b + 1], ALU.subtract, ALU.mult)
                ins_.then_inc(S["y_d"], 1)

            def largest(k):
                dve.wait_ge(S["y_a"], k + 1)
                dve.wait_ge(S["y_d"], k + 1)
                return v.tensor_reduce(ym[:, k:k + 1], y3[:, 4 * k:4 * k + 4, :].rearrange("p b d -> p (b d)"), AX.X,
                                       ALU.max, apply_absolute_value=True)

            statistics(0)
            statistics(1)
            roots(0, 2, 3)
            normalise(0)
            normalise(1)
            statistics(2)
            largest(0)
            statistics(3)
            dve.wait_ge(S["rs2_ready"], 1)
            normalise(2)
            roots(3, 4, 4)
            normalise(3)
            largest(1)
            largest(2)
            link(largest(3))
            v.reduce_max(am, ym, AX.X).then_inc(S["am_ready"], 1)
            filled(dve, "AM1", 0)
            v.reduce_max(a2, bank("AM1", 0)[0:1, 0:128], AX.X).then_inc(S["a1_ready"], 1)
            filled(dve, "AM2", 0)
            link(v.tensor_scalar(yb, bank("AM2", 0)[:, 0:1], 1e-8 / 32767.0, None, ALU.max))
            v.reciprocal(ysc, yb).then_inc(S["yq_scale"], 1)
            dve.wait_ge(S["yq_scale"], 1)
            dve.wait_ge(S["yt_ready"], 8)
            yt3 = qt.rearrange("p (h t) -> p h t", h=2)

            def y_round(c):
                v.tensor_scalar(scr[:, c, :].rearrange("p (h t) -> p h t", h=2), yt3[:, :, 512 * c:512 * c + 512],
                                ysc, MAGIC, ALU.mult, ALU.add).then_inc(S["yu_ready"], 1)

            def y_low(c):
                dve.wait_ge(S["yu_ready"], c + 1)
                v.tensor_tensor(ylo[:, :, 512 * c:512 * c + 512], scr16[:, c, :].rearrange("p (h t) -> p h t", h=2),
                                yhi[:, :, 512 * c:512 * c + 512], ALU.subtract).then_inc(S["yq_ready"], 1)

            y_round(0)
            dve.wait_ge(S["yhi_ready"], 2)
            y_low(0)
            link(v.tensor_scalar(yb, yb, 1.0 / 127.0, None, ALU.mult))
            v.tensor_scalar(sc1, wx, yb, None, ALU.mult).then_inc(S["ysc_ready"], 1)
            for c in range(1, 4):
                y_round(c)
                dve.wait_ge(S["yhi_ready"], c + 2)
                y_low(c)
            for n in range(16):
                c, f = n // 4, 2 * (n % 4)
                if n == 4:
                    filled(dve, "WG1", 0)
                    v.reduce_max(a1, bank("WG1", 0)[0:1, 0:128], AX.X).then_inc(S["wg_ready"], 1)
                if n == 8:
                    filled(dve, "WG2", 0)
                    link(v.tensor_copy(wg, bank("WG2", 0)[:, 0:1]))
                    link(v.reciprocal(rwg, wg))
                    v.tensor_scalar(rf, wom, rwg, None, ALU.mult).then_inc(S["rf_ready"], 1)
                for k in ((0, 2),) if n < 15 else ((0, 1), (1, 1)):
                    dve.wait_ge(S["h_ready"], 2 * n + k[0] + k[1])
                    ins_ = v.tensor_reduce(hm[:, n + k[0]:n + k[0] + 1], H[:, f + k[0]:f + k[0] + k[1], 512 * c:512 * c + 512],
                                           AX.XY, ALU.max, apply_absolute_value=True)
            link(ins_)
            v.reduce_max(am, hm, AX.X).then_inc(S["hm_ready"], 1)
            filled(dve, "HM1", 0)
            v.reduce_max(a3, bank("HM1", 0)[0:1, 0:128], AX.X).then_inc(S["ha_ready"], 1)
            filled(dve, "HM2", 0)
            link(v.tensor_scalar(hb, bank("HM2", 0)[:, 0:1], 1e-8 / 32767.0, None, ALU.max))
            link(v.reciprocal(hsc, hb))
            v.tensor_scalar(hrf, rf, hsc, None, ALU.mult).then_inc(S["hsc_ready"], 1)

            def rounded(n):
                if n >= 4:
                    dve.wait_ge(S["hq_ready"], n - 3)
                v.tensor_scalar(scr[:, n % 4, :], piece(H, n), hsc, MAGIC, ALU.mult, ALU.add).then_inc(S["hu_d"], 1)

            def low(n):
                f = n % 8
                dve.wait_ge(S["hhi_ready"], n + 1)
                dve.wait_ge(*rounded_by(n))
                part = (Hlo5 if f < 4 else Hlo8)[:, f % 4, 1024 * (n // 8):1024 * (n // 8) + 1024]
                v.scalar_tensor_tensor(out=part, in0=scr16[:, n % 4, :], scalar=rf[:, f:f + 1], in1=piece(Hhi, n),
                                       op0=ALU.mult, op1=ALU.subtract).then_inc(S["hq_ready"], 1)

            def final(i):
                filled(dve, "M2", i)
                v.scalar_tensor_tensor(out=xs[:, 512 * i:512 * i + 512], in0=bank("M2", i), scalar=sc2,
                                       in1=xs[:, 512 * i:512 * i + 512], op0=ALU.mult, op1=ALU.add)\
                 .then_inc(S["o_ready"], 1)

            rounded(0)
            link(v.tensor_scalar(sc2, hb, 1.0 / 127.0, None, ALU.mult))
            link(v.tensor_scalar(sc2, sc2, wg, None, ALU.mult))
            dve.wait_ge(S["x2b_ready"], 1)
            for n in range(16):
                if n + 1 in DVE_ROUNDS:
                    rounded(n + 1)
                low(n)
                if 9 <= n < 13:
                    final(n - 9)
            for i in range(4, 8):
                final(i)

        @block.tensor
        def _(pe):
            t = nc.tensor
            F = tb("F")

            def done(ins_):
                ins_.then_inc(S["pe"], 1)

            def keep_clock(i, n):
                o = take_bank(pe, "HT", i)
                for _ in range(n):
                    last = t.matmul(o[:, 0:256], ones[:].bitcast(bf16)[:, 0:128], ones[:].bitcast(bf16), start=True, stop=True)
                done(last)

            pe.wait_ge(S["ones_ready"], 1)
            keep_clock(0, 16)
            pe.wait_ge(S["ld_F"], 16)
            pe.wait_ge(ld_ctx[4], 16)
            for i in range(8):
                bq, h = i // 2, i % 2
                if h == 0:
                    pe.wait_ge(ld_ctx[bq], 16)
                o = take_bank(pe, "CD", i)
                for k in range(4):
                    if i == 0 and k == 2:
                        pe.wait_ge(ld_rest, 16)
                    b = 4 * bq + k
                    n = AF + 1 if b < TC - AF * NB else AF
                    last = t.matmul(o[:, 128 * k:128 * k + 128], cx[0:n, 256 * b + 128 * h:256 * b + 128 * h + 128],
                                    F[0:n, :], start=True, stop=True)
                done(last)
            pe.wait_ge(S["ld_wqk"], 32)
            o = take_bank(pe, "GG", 0)
            for h in range(2):
                for k in range(2):
                    last = t.matmul(o[:, 256 * h:256 * h + 256], wqT_s[:, k, 128 * h:128 * h + 128], wkT_s[:, k, :],
                                    start=(k == 0), stop=(k == 1))
            done(last)
            pe.wait_ge(S["bkb_ready"], 1)
            pe.wait_ge(S["ld_col"], 16)
            o = take_bank(pe, "SM", 0)
            for k in range(2):
                t.matmul(o[:, 0:D], bkb[:, k, :], wqT_s[:, k, :], start=(k == 0), stop=(k == 1))
            for h in range(2):
                for k in range(2):
                    t.matmul(o[:, D + h:D + h + 1], wkT_s[:, k, 128 * h:128 * h + 128], colv[:, 2 + k:3 + k],
                             start=(k == 0), stop=(k == 1))
            for k in range(2):
                last = t.matmul(o[:, D + 2:D + 3], bkb[:, k, :], colv[:, 2 + k:3 + k], start=(k == 0), stop=(k == 1))
            done(last)

            def vproj(i):
                o = take_bank(pe, "VP", i)
                for m in range(2):
                    for k in range(2):
                        c0 = 2048 * k + 128 * (2 * i + m)
                        last = t.matmul(o[:, 256 * m:256 * m + 256], ct[:, c0:c0 + 128], wvo[:, k, :],
                                        start=(k == 0), stop=(k == 1))
                done(last)

            for i in range(8):
                if i == 4:
                    pe.wait_ge(S["ld_wv"], 32)
                    o = take_bank(pe, "WVO", 0)
                    for h in range(2):
                        for k in range(2):
                            last = t.matmul(o[:, 256 * h:256 * h + 256], wvT_s[:, k, 128 * h:128 * h + 128], wo_s[:, k, :],
                                            start=(k == 0), stop=(k == 1))
                    done(last)
                bq, h = i // 2, i % 2
                if h == 0:
                    pe.wait_ge(S["xh_a" if bq % 2 else "xh_d"], bq // 2 + 1)
                o = take_bank(pe, "XD", i)
                for k in range(4):
                    b = 4 * bq + k
                    last = t.matmul(o[:, 128 * k:128 * k + 128], xh[:, 256 * b + 128 * h:256 * b + 128 * h + 128],
                                    F, start=True, stop=True)
                done(last)
            pe.wait_ge(S["bvb_ready"], 1)
            o = take_bank(pe, "BVO", 0)
            for k in range(2):
                last = t.matmul(o[:, 0:D], bvb[:, k, :], wo_s[:, k, :], start=(k == 0), stop=(k == 1))
            done(last)
            pe.wait_ge(S["wqk_ready"], 1)
            pe.wait_ge(S["xt_a"], 4)
            pe.wait_ge(S["xt_d"], 4)
            for i in range(8):
                h, c = i // 4, i % 4
                o = take_bank(pe, "QP", i)
                for k in range(2):
                    last = t.matmul(o, wqk[:, k, 128 * h:128 * h + 128], xt[:, 2048 * k + 512 * c:2048 * k + 512 * c + 512],
                                    start=(k == 0), stop=(k == 1))
                done(last)
            pe.wait_ge(S["ld_tab"], 16)
            pe.wait_ge(S["qb_ready"], 1)
            o = take_bank(pe, "QB1", 0)
            for r in range(2):
                last = t.matmul(o[0:NS, 16 * r:16 * r + 16], tb("FS")[:, NS * r:NS * r + NS], qb, start=True, stop=True)
            done(last)

            def gramian(i):
                pe.wait_ge(S["qt_ready"], 5 + i)
                o = take_bank(pe, "GR", i)
                for m in range(4):
                    g = 4 * i + m
                    for k in range(2):
                        c0 = 2048 * k + 128 * g
                        last = t.matmul(o[:, 128 * m:128 * m + 128], ct[:, c0:c0 + 128], qt[:, c0:c0 + 128],
                                        start=(k == 0), stop=(k == 1))
                done(last)

            def second_step(i):
                pe.wait_ge(S["gram_a"], i + 1)
                pe.wait_ge(S["gram_d"], i + 1)
                for g in range(4 * i, 4 * i + 4):
                    last = t.matmul(bank("UU", 0)[:, 32 * g:32 * g + 32], BU[:, g, :], gram[:, g, :], start=True, stop=True)
                return last

            pe.wait_ge(S["ct_ready"], 8)
            gramian(0)
            gramian(1)
            pe.wait_ge(S["ownq_ready"], 1)
            o = take_bank(pe, "QB2", 0)
            done(t.matmul(o, tb("JT", NS), ownq, start=True, stop=True))
            pe.wait_ge(S["bu_ready"], NJ)
            take_bank(pe, "UU", 0)
            second_step(0)
            gramian(2)
            second_step(1)
            gramian(3)
            second_step(2)
            done(second_step(3))
            pe.wait_ge(S["identb_ready"], 1)
            for h in range(2):
                o = take_bank(pe, "WB", h).bitcast(bf16)
                for f in range(8):
                    last = t.transpose(o[:, 128 * f:128 * f + 128], winq_t[:, f, 128 * h:128 * h + 128], identb[:])
                done(last)

            pe.wait_ge(S["wvo_ready"], 1)
            vproj(0)
            pe.wait_ge(S["ab_ready"], 1)
            o = take_bank(pe, "IN", 0)
            done(t.matmul(o[0:NS, :], tb("J"), pr2.rearrange("p g c -> p (g c)"), start=True, stop=True))
            vproj(1)
            pe.wait_ge(S["own_ready"], 1)
            o = take_bank(pe, "ME", 0)
            for r in range(2):
                last = t.matmul(o[:, 0:NB], tb("FR", NS)[:, 128 * r:128 * r + 128], ins[:, r:NM:2],
                                start=(r == 0), stop=(r == 1))
            done(last)
            pe.wait_ge(S["mean_ready"], 1)
            o = take_bank(pe, "TM", 0)
            done(t.transpose(o[0:NB, 0:128], mean, tb("I")))
            vproj(2)
            pe.wait_ge(S["cand_ready"], 1)
            o = take_bank(pe, "BC", 0)
            done(t.matmul(o[:, 0:256], ones[0:NB, :], cand, start=True, stop=True))
            vproj(3)
            pe.wait_ge(S["eq_ready"], 1)
            o = take_bank(pe, "EQ", 0)
            done(t.matmul(o[:, 0:1], tb("L"), eqrow, start=True, stop=True))
            vproj(4)
            pe.wait_ge(S["wn_ready"], 1)
            o = take_bank(pe, "W1", 0)
            for r in range(2):
                last = t.matmul(o[0:NS, 16 * r:16 * r + 16], tb("FS")[:, NS * r:NS * r + NS], wn, start=True, stop=True)
            done(last)
            pe.wait_ge(S["w1_ready"], 1)
            o = take_bank(pe, "W2", 0)
            done(t.matmul(o, tb("JT", NS), own, start=True, stop=True))
            vproj(5)
            vproj(6)

            def mix(*units):
                for i in units:
                    pe.wait_ge(S["nm_ready"], i // 2 + 1)
                    pe.wait_ge(S["nm_a"], i // 2 + 1)
                    o = take_bank(pe, "MX", i)
                    for m in range(4):
                        g = 4 * i + m
                        last = t.matmul(o[:, 128 * m:128 * m + 128], BUT[:, g, :], NM_[:, g, :], start=True, stop=True)
                    done(last)

            def attend(*units):
                for i in units:
                    pe.wait_ge(S["vh_ready"], i + 1)
                    pe.wait_ge(S["mix_ready"], i // 2 + 1)
                    o = take_bank(pe, "OO", i)
                    for m in range(2):
                        g = 2 * i + m
                        last = t.matmul(o[:, 256 * m:256 * m + 256], MIX[:, g, :], xh[:, 256 * g:256 * g + 256],
                                        start=True, stop=True)
                    done(last)

            pe.wait_ge(S["nz_ready"], 1)
            pe.wait_ge(S["bt_ready"], NJ)
            mix(0, 1)
            vproj(7)
            attend(0, 1)
            mix(2, 3)
            attend(2, 3, 4, 5, 6, 7)

            def open_sums(lo, hi):
                for i in range(lo, hi):
                    pe.wait_ge(ld_xs[i // 2], 16)
                    t.matmul(take_bank(pe, "IV", i), tb("I"), xs[:, 512 * i:512 * i + 512], start=True, stop=False)

            open_sums(OPENED, 8)
            for i in range(8):
                pe.wait_ge(spec_in[i], 32 if i % 2 else 16)
            for i in range(4):
                pe.wait_ge(spec_sw[i], 16)
            for i in range(8):
                o = take_bank(pe, "IV", i) if i < OPENED else bank("IV", i)
                done(t.matmul(o, tb("FT"), ct[:, 512 * i:512 * i + 512], start=(i < OPENED), stop=True))
            for i in range(8):
                pe.wait_ge(S["y_a"], i // 2 + 1)
                pe.wait_ge(S["y_d"], i // 2 + 1)
                o = take_bank(pe, "TY", i)
                for h in range(2):
                    for m in range(2):
                        b = 2 * i + m
                        last = t.transpose(o[:, 256 * h + 128 * m:256 * h + 128 * m + 128],
                                           yn[:, 256 * b + 128 * h:256 * b + 128 * h + 128], tb("I"))
                done(last)
                if i % 2:
                    keep_clock(1 + i // 2, (20, 12, 6, 4)[i // 2])
            pe.wait_ge(S["am_ready"], 1)
            o = take_bank(pe, "AM1", 0)
            done(t.transpose(o[0:1, 0:128], am, tb("I")))
            pe.wait_ge(S["a1_ready"], 1)
            o = take_bank(pe, "AM2", 0)
            done(t.matmul(o[:, 0:1], inv[:], a2, start=True, stop=True))
            keep_clock(5, 8)
            pe.wait_ge(S["winq_ready"], 2)

            def hidden_units(n, count, c, f):
                o = [take_bank(pe, "M1", n + k) for k in range(count)]
                for h in range(2):
                    pe.wait_ge(S["yhi_ready"], h + 1 if c == 0 else c + 2)
                    for k in range(count):
                        fs = slice(128 * (f + k), 128 * (f + k) + 128)
                        t.matmul(o[k], winq[:, h, fs], yhi[:, h, 512 * c:512 * c + 512], start=(h == 0), stop=False)
                pe.wait_ge(S["yq_ready"], c + 1)
                for k in range(count):
                    for h in range(2):
                        fs = slice(128 * (f + k), 128 * (f + k) + 128)
                        last = t.matmul(o[k], winq[:, h, fs], ylo[:, h, 512 * c:512 * c + 512], start=False, stop=(h == 1))
                    done(last)

            hidden_units(0, 4, 0, 0)
            for n in range(4, 32):
                if n == 8:
                    pe.wait_ge(S["wom_ready"], 1)
                    o = take_bank(pe, "WG1", 0)
                    done(t.transpose(o[0:1, 0:128], wg, tb("I")))
                if n == 16:
                    pe.wait_ge(S["wg_ready"], 1)
                    o = take_bank(pe, "WG2", 0)
                    done(t.matmul(o[:, 0:1], ones[0:1, :], a1, start=True, stop=True))
                hidden_units(n, 1, n // 8, n % 8)
            keep_clock(6, 16)
            pe.wait_ge(S["hm_ready"], 1)
            o = take_bank(pe, "HM1", 0)
            done(t.transpose(o[0:1, 0:128], am, tb("I")))
            pe.wait_ge(S["ha_ready"], 1)
            o = take_bank(pe, "HM2", 0)
            done(t.matmul(o[:, 0:1], inv[:], a3, start=True, stop=True))
            keep_clock(7, 8)

            def product(o, k, part, c, f, start=False, stop=False):
                t0 = 128 * (8 * c + k)
                return t.matmul(o[k // 2][:, 256 * (k % 2):256 * (k % 2) + 256], part[:, t0:t0 + 128], woutq[:, f, :],
                                start=start, stop=stop)

            for c in range(2):
                o = [take_bank(pe, "M2", 4 * c + k) for k in range(4)]

                def high_products(f):
                    if c == 0 and f == 0:
                        pe.wait_ge(S["hhi_first"], 1)
                    else:
                        pe.wait_ge(S["hhi_ready"], 8 * c + f + 1)
                    for k in range(8):
                        if c == 0 and f == 0 and k == 4:
                            pe.wait_ge(S["hhi_ready"], 1)
                        product(o, k, Hhi[:, f], c, f, start=(f == 0 and k % 2 == 0))

                def low_products(f):
                    pe.wait_ge(S["hq_ready"], 8 * c + f + 1)
                    for k in range(8):
                        product(o, k, (Hlo5 if f < 4 else Hlo8)[:, f % 4], c, f)

                high_products(0)
                for f in range(1, 7):
                    high_products(f)
                    low_products(f - 1)
                low_products(6)
                pe.wait_ge(S["hhi_ready"], 8 * c + 8)
                pe.wait_ge(S["hq_ready"], 8 * c + 8)
                for k in range(8):
                    product(o, k, Hhi[:, 7], c, 7)
                    last = product(o, k, Hlo8[:, 3], c, 7, stop=(k % 2 == 1))
                    if k % 2:
                        done(last)


def kernel(x, ctx_1024, L0_xattn_Wq, L0_xattn_bq, L0_xattn_Wk, L0_xattn_bk, L0_xattn_Wv, L0_xattn_bv,
           L0_xattn_Wo, L0_xattn_bo, L0_ffn_W_in, L0_ffn_b_in, L0_ffn_W_out, L0_ffn_b_out):
    import concourse.bacc as bacc
    from concourse.bass_utils import run_bass_kernel_spmd

    def cols(v):
        return np.asarray(v).reshape(-1, 128).T

    tab, at = shape_tables()
    arrays = {
        "x": x, "ctx_in": ctx_1024, "wqT": np.asarray(L0_xattn_Wq).T, "wkT": np.asarray(L0_xattn_Wk).T,
        "wvT": np.asarray(L0_xattn_Wv).T,
        "wo": L0_xattn_Wo, "winT": np.asarray(L0_ffn_W_in).T, "wout": L0_ffn_W_out,
        "cols": np.concatenate([cols(L0_xattn_bk), cols(L0_xattn_bq), cols(L0_xattn_bv), cols(L0_ffn_b_in)], 1),
        "rows": np.concatenate([np.asarray(L0_xattn_bo), np.asarray(L0_ffn_b_out)])[None],
        "tab": tab,
    }
    arrays = {k: np.ascontiguousarray(v) for k, v in arrays.items()}
    nc = bacc.Bacc("TRN2", target_bir_lowering=False, num_devices=1)
    aps = {k: nc.dram_tensor(k + "_dram", v.shape, mybir.dt.from_np(v.dtype), kind="ExternalInput").ap()
           for k, v in arrays.items()}
    out = nc.dram_tensor("out_dram", (1, T, D), mybir.dt.float32, kind="ExternalOutput").ap()
    build(nc, out=out, at=at, **aps)
    r = run_bass_kernel_spmd(nc, [{k + "_dram": v for k, v in arrays.items()}], core_ids=[0])
    return r.results[0]["out_dram"]
```
